# Optimizing a Trainium2 kernel written in Bass

```python
import numpy as np
import jax
import jax.numpy as jnp

def _softmax(x, axis=-1):
    return jax.nn.softmax(x, axis=axis)

def _gelu(x):
    return jax.nn.gelu(x, approximate=True)

def _silu(x):
    return jax.nn.silu(x)

def _sigmoid(x):
    return jax.nn.sigmoid(x)

def _layernorm(x, axis=-1, eps=1e-05):
    m = jnp.mean(x, axis=axis, keepdims=True)
    v = jnp.var(x, axis=axis, keepdims=True)
    return (x - m) / jnp.sqrt(v + eps)

def _scatter_add(tgt, idx, src, axis=0):
    return tgt.at[idx].add(src)

def _segment_sum(src, seg, n):
    return jax.ops.segment_sum(src, seg, n)
kernel_name = 'mk_vit_tower_cls_d1_tok_img768_r4_fb1fb8'

def setup_inputs(seed: int=0):
    np.random.seed(seed)
    _w = jnp.asarray

    def _rec_inputs():
        import jax
        import jax.numpy as jnp
        _rk = jax.random.key(seed)
        x = -0.00016672 + 0.999947 * jax.random.normal(jax.random.fold_in(_rk, 1), (16, 3, 96, 96), jnp.float32)
        cls_tok = 0.02 * jax.random.normal(jax.random.fold_in(_rk, 5), (1, 1, 192), jnp.float32)
        return (x, cls_tok)
    x, cls_tok = _rec_inputs()

    def _L0_tok_setup():
        import jax, jax.numpy as jnp
        import numpy as np
        IMG_SIZE = 96
        PATCH = 16
        LATENT = 192
        N_PATCHES = (IMG_SIZE // PATCH) ** 2
        LIN_IN = PATCH * PATCH * 3

        def _patchify(x):
            B, C, H, Wd = x.shape
            Hp, Wp = (H // PATCH, Wd // PATCH)
            x = x.reshape(B, C, Hp, PATCH, Wp, PATCH)
            x = x.transpose(0, 2, 4, 1, 3, 5)
            return x.reshape(B, Hp * Wp, C * PATCH * PATCH)
        key = jax.random.key(seed)
        k1, k2, k3, k4, k5 = jax.random.split(key, 5)
        B = 64
        x = jax.random.normal(k1, (B, 3, IMG_SIZE, IMG_SIZE), dtype=jnp.float32)
        lim = 1.0 / np.sqrt(LIN_IN)
        W = jax.random.uniform(k2, (LATENT, LIN_IN), minval=-lim, maxval=lim, dtype=jnp.float32)
        b = jax.random.uniform(k3, (LATENT,), minval=-lim, maxval=lim, dtype=jnp.float32)
        class_token = jax.random.normal(k4, (1, 1, LATENT), dtype=jnp.float32) * 0.02
        pos_embedding = jax.random.normal(k5, (1, N_PATCHES + 1, LATENT), dtype=jnp.float32) * 0.02
        return {'x': x, 'W': W, 'b': b, 'class_token': class_token, 'pos_embedding': pos_embedding}
    _L0_tok_all = _L0_tok_setup()
    _L0_tok_in = {k: v for k, v in _L0_tok_all.items() if k in ('W', 'b', 'class_token', 'pos_embedding')}
    del _L0_tok_all

    def _L0_attn_setup():
        import jax, jax.numpy as jnp
        import numpy as np
        D_MODEL = 192
        D_STATE = 16
        D_CONV = 4
        EXPAND = 2
        D_INNER = EXPAND * D_MODEL
        DT_RANK = (D_MODEL + 15) // 16
        BATCH = 2
        SEQLEN = 256

        def _mamba(x, in_w, conv_w, conv_b, xproj_w, dt_w, dt_b, A_log, Dp, out_w):
            B, L, _ = x.shape
            xz = x @ in_w.T
            xc, z = jnp.split(xz, 2, axis=-1)
            K = conv_w.shape[1]
            xpad = jnp.pad(xc, ((0, 0), (K - 1, 0), (0, 0)))
            xconv = conv_b + sum((conv_w[:, k] * xpad[:, k:k + L, :] for k in range(K)))
            u = jax.nn.silu(xconv)
            proj = u @ xproj_w.T
            dt_rank = dt_w.shape[1]
            n = A_log.shape[1]
            dtx, Bm, Cm = jnp.split(proj, [dt_rank, dt_rank + n], axis=-1)
            dt = jax.nn.softplus(dtx @ dt_w.T + dt_b)
            A = -jnp.exp(A_log)
            dA = jnp.exp(dt[..., None] * A)
            dBu = dt[..., None] * Bm[:, :, None, :] * u[..., None]

            def step(h, inp):
                dA_t, dBu_t, C_t = inp
                h = dA_t * h + dBu_t
                y = jnp.einsum('bdn,bn->bd', h, C_t)
                return (h, y)
            h0 = jnp.zeros((B, u.shape[-1], n), x.dtype)
            _, ys = jax.lax.scan(step, h0, (dA.transpose(1, 0, 2, 3), dBu.transpose(1, 0, 2, 3), Cm.transpose(1, 0, 2)))
            y = ys.transpose(1, 0, 2) + u * Dp
            y = y * jax.nn.silu(z)
            return y @ out_w.T
        key = jax.random.key(seed)
        ks = jax.random.split(key, 10)
        s = 0.02
        f32 = jnp.float32
        x = jax.random.normal(ks[0], (BATCH, SEQLEN, D_MODEL), f32)
        bm_in_w = jax.random.normal(ks[1], (2 * D_MODEL, D_MODEL), f32) * s
        bm_in_b = jnp.zeros((2 * D_MODEL,), f32)
        bm_out_w = jax.random.normal(ks[2], (D_MODEL, D_MODEL), f32) * s
        bm_out_b = jnp.zeros((D_MODEL,), f32)
        m_in_w = jax.random.normal(ks[3], (2 * D_INNER, D_MODEL), f32) * s
        m_conv_w = jax.random.normal(ks[4], (D_INNER, D_CONV), f32) * s
        m_conv_b = jnp.zeros((D_INNER,), f32)
        m_xproj_w = jax.random.normal(ks[5], (DT_RANK + 2 * D_STATE, D_INNER), f32) * s
        m_dt_w = jax.random.normal(ks[6], (D_INNER, DT_RANK), f32) * s
        m_dt_b = jnp.full((D_INNER,), -4.6, f32)
        m_A_log = jnp.log(jnp.broadcast_to(jnp.arange(1, D_STATE + 1, dtype=f32), (D_INNER, D_STATE)))
        m_D = jnp.ones((D_INNER,), f32)
        m_out_w = jax.random.normal(ks[7], (D_MODEL, D_INNER), f32) * s
        ln_g = jnp.ones((D_MODEL,), f32)
        ln_b = jnp.zeros((D_MODEL,), f32)
        return {'x': x, 'bm_in_w': bm_in_w, 'bm_in_b': bm_in_b, 'bm_out_w': bm_out_w, 'bm_out_b': bm_out_b, 'm_in_w': m_in_w, 'm_conv_w': m_conv_w, 'm_conv_b': m_conv_b, 'm_xproj_w': m_xproj_w, 'm_dt_w': m_dt_w, 'm_dt_b': m_dt_b, 'm_A_log': m_A_log, 'm_D': m_D, 'm_out_w': m_out_w, 'ln_g': ln_g, 'ln_b': ln_b}
    _L0_attn_all = _L0_attn_setup()
    _L0_attn_in = {k: v for k, v in _L0_attn_all.items() if k in ('bm_in_w', 'bm_in_b', 'bm_out_w', 'bm_out_b', 'm_in_w', 'm_conv_w', 'm_conv_b', 'm_xproj_w', 'm_dt_w', 'm_dt_b', 'm_A_log', 'm_D', 'm_out_w', 'ln_g', 'ln_b')}
    del _L0_attn_all

    def _L0_ffn_setup():
        import jax, jax.numpy as jnp
        import numpy as np
        B, T, H, F, E = (128, 32, 192, 768, 3)
        key = jax.random.key(seed)
        ks = jax.random.split(key, 4)
        s = 0.02
        return {'x': jax.random.normal(ks[0], (B, T, H), jnp.float32), 'Wg': jax.random.normal(ks[1], (E, H), jnp.float32) * s, 'W1': jax.random.normal(ks[2], (E, H, F), jnp.float32) * s, 'b1': jnp.zeros((E, F), jnp.float32), 'W2': jax.random.normal(ks[3], (E, F, H), jnp.float32) * s, 'b2': jnp.zeros((E, H), jnp.float32)}
    _L0_ffn_all = _L0_ffn_setup()
    _L0_ffn_in = {k: v for k, v in _L0_ffn_all.items() if k in ('Wg', 'W1', 'b1', 'W2', 'b2')}
    del _L0_ffn_all
    return {'x': x, 'cls_tok': cls_tok, 'L0_tok_W': _L0_tok_in['W'], 'L0_tok_b': _L0_tok_in['b'], 'L0_tok_class_token': _L0_tok_in['class_token'], 'L0_tok_pos_embedding': _L0_tok_in['pos_embedding'], 'L0_attn_bm_in_w': _L0_attn_in['bm_in_w'], 'L0_attn_bm_in_b': _L0_attn_in['bm_in_b'], 'L0_attn_bm_out_w': _L0_attn_in['bm_out_w'], 'L0_attn_bm_out_b': _L0_attn_in['bm_out_b'], 'L0_attn_m_in_w': _L0_attn_in['m_in_w'], 'L0_attn_m_conv_w': _L0_attn_in['m_conv_w'], 'L0_attn_m_conv_b': _L0_attn_in['m_conv_b'], 'L0_attn_m_xproj_w': _L0_attn_in['m_xproj_w'], 'L0_attn_m_dt_w': _L0_attn_in['m_dt_w'], 'L0_attn_m_dt_b': _L0_attn_in['m_dt_b'], 'L0_attn_m_A_log': _L0_attn_in['m_A_log'], 'L0_attn_m_D': _L0_attn_in['m_D'], 'L0_attn_m_out_w': _L0_attn_in['m_out_w'], 'L0_attn_ln_g': _L0_attn_in['ln_g'], 'L0_attn_ln_b': _L0_attn_in['ln_b'], 'L0_ffn_Wg': _L0_ffn_in['Wg'], 'L0_ffn_W1': _L0_ffn_in['W1'], 'L0_ffn_b1': _L0_ffn_in['b1'], 'L0_ffn_W2': _L0_ffn_in['W2'], 'L0_ffn_b2': _L0_ffn_in['b2']}

def reference(x, cls_tok, L0_tok_W, L0_tok_b, L0_tok_class_token, L0_tok_pos_embedding, L0_attn_bm_in_w, L0_attn_bm_in_b, L0_attn_bm_out_w, L0_attn_bm_out_b, L0_attn_m_in_w, L0_attn_m_conv_w, L0_attn_m_conv_b, L0_attn_m_xproj_w, L0_attn_m_dt_w, L0_attn_m_dt_b, L0_attn_m_A_log, L0_attn_m_D, L0_attn_m_out_w, L0_attn_ln_g, L0_attn_ln_b, L0_ffn_Wg, L0_ffn_W1, L0_ffn_b1, L0_ffn_W2, L0_ffn_b2):
    import jax
    import jax.numpy as jnp

    def _L0_tok_ref(x, W, b, class_token, pos_embedding):
        import jax, jax.numpy as jnp
        import numpy as np
        IMG_SIZE = 96
        PATCH = 16
        LATENT = 192
        N_PATCHES = (IMG_SIZE // PATCH) ** 2
        LIN_IN = PATCH * PATCH * 3

        def _patchify(x):
            B, C, H, Wd = x.shape
            Hp, Wp = (H // PATCH, Wd // PATCH)
            x = x.reshape(B, C, Hp, PATCH, Wp, PATCH)
            x = x.transpose(0, 2, 4, 1, 3, 5)
            return x.reshape(B, Hp * Wp, C * PATCH * PATCH)
        patches = _patchify(x)
        proj = jnp.einsum('bld,ed->ble', patches, W) + b
        B = proj.shape[0]
        cls = jnp.broadcast_to(class_token, (B, 1, LATENT))
        out = jnp.concatenate([cls, proj], axis=1)
        return out + pos_embedding

    def _L0_attn_ref(x, bm_in_w, bm_in_b, bm_out_w, bm_out_b, m_in_w, m_conv_w, m_conv_b, m_xproj_w, m_dt_w, m_dt_b, m_A_log, m_D, m_out_w, ln_g, ln_b):
        import jax, jax.numpy as jnp
        import numpy as np
        D_MODEL = 192
        D_STATE = 16
        D_CONV = 4
        EXPAND = 2
        D_INNER = EXPAND * D_MODEL
        DT_RANK = (D_MODEL + 15) // 16
        BATCH = 2
        SEQLEN = 256

        def _mamba(x, in_w, conv_w, conv_b, xproj_w, dt_w, dt_b, A_log, Dp, out_w):
            B, L, _ = x.shape
            xz = x @ in_w.T
            xc, z = jnp.split(xz, 2, axis=-1)
            K = conv_w.shape[1]
            xpad = jnp.pad(xc, ((0, 0), (K - 1, 0), (0, 0)))
            xconv = conv_b + sum((conv_w[:, k] * xpad[:, k:k + L, :] for k in range(K)))
            u = jax.nn.silu(xconv)
            proj = u @ xproj_w.T
            dt_rank = dt_w.shape[1]
            n = A_log.shape[1]
            dtx, Bm, Cm = jnp.split(proj, [dt_rank, dt_rank + n], axis=-1)
            dt = jax.nn.softplus(dtx @ dt_w.T + dt_b)
            A = -jnp.exp(A_log)
            dA = jnp.exp(dt[..., None] * A)
            dBu = dt[..., None] * Bm[:, :, None, :] * u[..., None]

            def step(h, inp):
                dA_t, dBu_t, C_t = inp
                h = dA_t * h + dBu_t
                y = jnp.einsum('bdn,bn->bd', h, C_t)
                return (h, y)
            h0 = jnp.zeros((B, u.shape[-1], n), x.dtype)
            _, ys = jax.lax.scan(step, h0, (dA.transpose(1, 0, 2, 3), dBu.transpose(1, 0, 2, 3), Cm.transpose(1, 0, 2)))
            y = ys.transpose(1, 0, 2) + u * Dp
            y = y * jax.nn.silu(z)
            return y @ out_w.T
        mparams = (m_in_w, m_conv_w, m_conv_b, m_xproj_w, m_dt_w, m_dt_b, m_A_log, m_D, m_out_w)
        xp = x @ bm_in_w.T + bm_in_b
        x_f, x_b = jnp.split(xp, 2, axis=-1)
        out_f = _mamba(x_f, *mparams)
        out_b = jnp.flip(_mamba(jnp.flip(x_b, axis=1), *mparams), axis=1)
        mo = (out_f + out_b) @ bm_out_w.T + bm_out_b
        h = mo + x
        mu = jnp.mean(h, axis=-1, keepdims=True)
        var = jnp.mean(jnp.square(h - mu), axis=-1, keepdims=True)
        return (h - mu) * jax.lax.rsqrt(var + 1e-05) * ln_g + ln_b

    def _L0_ffn_ref(x, Wg, W1, b1, W2, b2):
        import jax, jax.numpy as jnp
        import numpy as np
        B, T, H, F, E = (128, 32, 192, 768, 3)
        scores = jax.nn.softmax(jnp.mean(x, axis=1) @ Wg.T, axis=-1)
        _, idx = jax.lax.top_k(scores, 1)
        sel = idx[:, 0]
        h = jax.nn.gelu(jnp.einsum('bth,ehf->betf', x, W1) + b1[None, :, None, :], approximate=False)
        y = jnp.einsum('betf,efh->beth', h, W2) + b2[None, :, None, :]
        w = scores * jax.nn.one_hot(sel, E, dtype=scores.dtype)
        out = jnp.einsum('beth,be->bth', y, w)
        return out
    h = _L0_tok_ref(x, L0_tok_W, L0_tok_b, L0_tok_class_token, L0_tok_pos_embedding)
    h = jnp.concatenate([jnp.broadcast_to(cls_tok, (h.shape[0], 1, h.shape[2])), h], axis=1)
    h = h + _L0_attn_ref(_layernorm(h, axis=-1), L0_attn_bm_in_w, L0_attn_bm_in_b, L0_attn_bm_out_w, L0_attn_bm_out_b, L0_attn_m_in_w, L0_attn_m_conv_w, L0_attn_m_conv_b, L0_attn_m_xproj_w, L0_attn_m_dt_w, L0_attn_m_dt_b, L0_attn_m_A_log, L0_attn_m_D, L0_attn_m_out_w, L0_attn_ln_g, L0_attn_ln_b)
    h = h + _L0_ffn_ref(_layernorm(h, axis=-1), L0_ffn_Wg, L0_ffn_W1, L0_ffn_b1, L0_ffn_W2, L0_ffn_b2)
    return h

_drawn_inputs = setup_inputs


def setup_inputs(seed=0):
    import zlib

    import numpy as np

    out = dict(_drawn_inputs(seed))
    spreads = {'L0_attn_bm_in_b': (0.0, 0.8),
     'L0_attn_bm_out_b': (0.0, 0.1),
     'L0_attn_m_conv_b': (0.0, 0.8),
     'L0_attn_m_dt_b': (-4.599999904632568, 0.6),
     'L0_attn_m_D': (1.0, 0.6),
     'L0_attn_ln_g': (1.0, 0.2),
     'L0_attn_ln_b': (0.0, 0.1),
     'L0_ffn_b1': (0.0, 0.8),
     'L0_ffn_b2': (0.0, 0.389)}
    factors = {'L0_attn_bm_in_w': 8.0,
     'L0_attn_bm_out_w': 8.0,
     'L0_attn_m_in_w': 8.0,
     'L0_attn_m_conv_w': 8.0,
     'L0_attn_m_xproj_w': 8.0,
     'L0_attn_m_dt_w': 8.0,
     'L0_attn_m_A_log': 8.0,
     'L0_attn_m_out_w': 8.0,
     'L0_ffn_W1': 3.206,
     'L0_ffn_W2': 2.941}
    for name, (base, spread) in spreads.items():
        noise = np.random.default_rng([zlib.crc32(name.encode()), seed]).standard_normal(out[name].shape)
        drawn = base * np.exp(spread * noise) if base else spread * noise
        out[name] = jnp.asarray(drawn.astype(out[name].dtype))
    for name, factor in factors.items():
        out[name] = (out[name] * factor).astype(out[name].dtype)
    return out
```

```python
import concourse.bass as bass
from concourse import mybir
from contextlib import ExitStack

BATCH, LEN, DIM = 16, 38, 192
HALF = DIM // 2
PATCHES, PATCH_DIM = 36, 768
INNER, STATE, TAPS, DT_RANK = 384, 16, 4, 12
CHUNKS = INNER // 128
EXPERTS, HIDDEN = 3, 768
GROUP = 4
GROUPS = BATCH // GROUP
TOK = GROUP * LEN
SEQS = 2 * GROUP
STOK = SEQS * LEN
PK = PATCH_DIM // 128
NH = STATE // 2
UNITS = 2 * CHUNKS
FT = EXPERTS * HIDDEN // 128
FPE = HIDDEN // 128
BCR = 2 * STATE
XPO = 3 * BCR + DT_RANK
BLOCKS = [(0, 3 * LEN), (3 * LEN, 3 * LEN), (6 * LEN, 2 * LEN)]
LN_EPS = 1e-5

S_POS, S_TOKB, S_CLS, S_CT, S_INB, S_OUTB, S_LNG, S_LNB, S_WG, S_B2, S_END = 0, 74, 76, 78, 80, 84, 86, 88, 90, 96, 102
C_CW, C_CB, C_DTB, C_ALOG, C_D, C_B1, C_END = 0, 12, 15, 18, 66, 69, 87
K_ID, K_CD, K_CO, K_J, K_ONE, K_END = 0, 128, 224, 320, 416, 544


def tower(nc, xp, tokw, small96, small128, consts, sel, w_in, w_min, w_xp, w_dt, w_out, w_bmo, w1, w2, out):
    f32, bf16 = mybir.dt.float32, mybir.dt.bfloat16
    ALU, ACT, AX = mybir.AluOpType, mybir.ActivationFunctionType, mybir.AxisListType
    with ExitStack() as ctx:
        def sb(name, shape, dt=f32):
            return ctx.enter_context(nc.sbuf_tensor(name, shape, dt))

        def sem(name):
            return ctx.enter_context(nc.semaphore(name))

        tokw_s = sb("tokw_s", [128, PK, DIM])
        s96 = sb("s96", [HALF, S_END])
        s128 = sb("s128", [128, C_END])
        cst = sb("cst", [128, K_END])
        sel_s = sb("sel_s", [3 * BCR, BCR], bf16)
        win_s = sb("win_s", [HALF, 2, 2 * DIM])
        wmin_s = sb("wmin_s", [HALF, 2, 2 * INNER])
        wxp_s = sb("wxp_s", [128, CHUNKS, XPO])
        wdt_s = sb("wdt_s", [128, INNER])
        w1_s = sb("w1_s", [HALF, 2, EXPERTS * HIDDEN])
        w2_s = sb("w2_s", [128, FT, DIM])
        ident = cst[:, K_ID:K_ID + 128]
        posf = sb("posf", [HALF, 2, LEN])
        eps = sb("eps", [128, 1])
        Aneg = sb("Aneg", [128, CHUNKS * STATE])
        diag = sb("diag", [128, CHUNKS, TAPS, 128])
        wf = sb("wf", [128, CHUNKS, DIM])
        patches = sb("patches", [128, PK, GROUP * PATCHES])
        h0 = sb("h0", [HALF, 2, 2, TOK])
        xc1 = sb("xc1", [HALF, 2, TOK])
        sq1 = sb("sq1", [HALF, 2, TOK])
        rs1 = sq1
        xin = sb("xin", [HALF, 2, 2, TOK])
        xfb = sb("xfb", [HALF, 2, 2, GROUP, LEN])
        xpad = sb("xpad", [128, CHUNKS, SEQS, LEN + TAPS - 1])
        u = sb("u", [128, 2, CHUNKS, STOK])
        sz = sb("sz", [128, 2, CHUNKS, STOK])
        dt = sb("dt", [128, CHUNKS, STOK])
        du = sb("du", [128, CHUNKS, STOK])
        shared = sb("shared", [128, FT * TOK])
        hid = shared[:].rearrange("p (f t) -> p f t", f=FT)
        sp3 = shared[:].rearrange("p (k c t) -> p k c t", k=3, c=CHUNKS)
        spe, spl, spi = sp3[:, 0], sp3[:, 1], sp3[:, 2]
        wout_s = shared[0:HALF, 0:2 * INNER].rearrange("p (k n) -> p k n", k=2)
        wbmo_s = shared[0:HALF, 2 * INNER:2 * INNER + 2 * DIM].rearrange("p (k n) -> p k n", k=2)
        bcf = sb("bcf", [XPO, STOK])
        bc3 = sb("bc3", [3 * BCR, STOK], bf16)
        bcm = sb("bcm", [3 * BCR, STOK], bf16)
        BC = sb("BC", [128, 2, 2 * NH, STOK])
        AB = 3
        a = sb("a", [128, AB, NH, SEQS, LEN])
        HB = 2
        hb = sb("hb", [128, HB, NH, STOK])
        yTs = sb("yTs", [128, 3, 128])
        yg = sb("yg", [128, STOK])
        ys = sb("ys", [128, CHUNKS, TOK])
        h1 = sb("h1", [HALF, 2, TOK])
        xc2 = h1
        sq2 = sb("sq2", [HALF, 2, TOK])
        rs2 = sq2
        h2 = sb("h2", [HALF, 2, TOK])
        t2 = sb("t2", [HALF, 2, TOK])
        tm = sb("tm", [HALF, 2, GROUP])
        tmw = sb("tmw", [HALF, 2, GROUP, EXPERTS])
        gl = sb("gl", [128, GROUP, EXPERTS])
        gm = sb("gm", [128, GROUP, 4])
        ge_ = sb("ge_", [128, GROUP, EXPERTS])
        wg = sb("wg", [128, GROUP, EXPERTS])
        b2w = sb("b2w", [HALF, 2, GROUP, EXPERTS])
        b2s = sb("b2s", [HALF, 2, GROUP])
        res = t2

        FR = [ctx.enter_context(nc.psum_tensor(f"FR{i}", [128, 512], f32)) for i in range(3)]
        BR = [ctx.enter_context(nc.psum_tensor(f"BR{i}", [128, 512], f32)) for i in range(2)]
        YT = [ctx.enter_context(nc.psum_tensor(f"YT{i}", [128, 3, 128], f32)) for i in range(CHUNKS)]

        ld_tok, ld_mix, ld_out, ld_ffn = sem("ld_tok"), sem("ld_mix"), sem("ld_out"), sem("ld_ffn")
        ld_patch = sem("ld_patch")
        fr_full = [sem(f"fr_full{i}") for i in range(3)]
        fr_free = [sem(f"fr_free{i}") for i in range(3)]
        br_full = [sem(f"br_full{i}") for i in range(2)]
        br_free = [sem(f"br_free{i}") for i in range(2)]
        names = """posf_made consts_made pads_made a_log_exp a_made wf_full wf_made wf_free patch_used
        h0_made xc1_made rln1 rs1_made xin_made xfb_made xpad_made u_made sz_made dtx_made bcf_made
        sp_abs sp_exp sp_log sp_parts bc_split dt_made du_made B_made pool_chain a_ready b_made h_made p_made
        yT_full yT_copied yT_turned y_skip y_gated ys_made h1_made xc2_made rln2 rs2_made h2_made t2_made
        mo_made tmw_made gate_exp gate_in w_made hid_raw hid_made res_made out_done dve_chain h2b_made""".split()
        s = {n: sem(n) for n in names}

        F_TILES = 18 + BCR
        B_TILES = 3 + 5 + 1 + 6 + 1

        T_H, T_C1, T_V1, T_XF, T_XC, T_CONV, T_Z, T_XP, T_DT, T_BC = 0, 1, 2, 3, 5, 8, 11, 14, 15, 18
        T_Y, T_MO, T_C2, T_V2, T_C3, T_V3, T_G, T_UP, T_O = 0, 3, 4, 5, 6, 7, 8, 9, 15

        SLOTS = [[("du2", 0), ("bc1", 0), ("y2", -1), ("b_mo", -1)],
                 [("b_ln", -1), ("f_tok", 1)],
                 [("f_in", 1), ("b_ln2", -1), ("f_xc", 1)],
                 [("f_conv", 1), ("f_dt", 1), ("b_gate", -1)],
                 [("du0", 1), ("bc0", 1), ("y0", 0), ("b_up", -1)],
                 [("du1", 1), ("y1", 0), ("b_out", -1)]]

        PROLOGUE = ("f_tok", "f_in", "f_xc", "f_conv", "f_dt", "bc0", "du0", "du1")
        F_FILLS = {"f_tok": [T_H, T_C1, T_V1], "f_in": [T_XF, T_XF + 1],
                   "f_xc": [T_XC + c for c in range(CHUNKS)],
                   "f_conv": [T_CONV + c for c in range(CHUNKS)] + [T_Z + c for c in range(CHUNKS)],
                   "f_dt": [T_XP] + [T_DT + c for c in range(CHUNKS)],
                   "bc0": [T_BC + j for j in range(2 * NH)], "bc1": [T_BC + 2 * NH + j for j in range(2 * NH)]}
        B_FILLS = {"y0": [T_Y], "y1": [T_Y + 1], "y2": [T_Y + 2], "b_mo": [T_MO], "b_ln": [T_C2, T_V2],
                   "b_ln2": [T_C3, T_V3], "b_gate": [T_G], "b_up": [T_UP + i for i in range(FT // 3)], "b_out": [T_O]}

        def fills_before(fills, banks):
            order = [(st, 0) for st in PROLOGUE]
            order += [(st, g + d) for g in range(GROUPS + 1) for slot in SLOTS for st, d in slot if 0 <= g + d < GROUPS]
            count, before = [0] * banks, {}
            for st, g in order:
                for i in fills.get(st, []):
                    before[g, i] = count[i % banks]
                    count[i % banks] += 1
            return before

        F_BEFORE, B_BEFORE = fills_before(F_FILLS, 3), fills_before(B_FILLS, 2)

        def f_before(g, i):
            return F_BEFORE[g, i]

        def b_before(g, i):
            return B_BEFORE[g, i]

        def program(unit, stages, ahead=None):
            for st in PROLOGUE:
                if st in stages:
                    stages[st](0)
            if ahead:
                ahead(0)
                ahead(1)
            for g in range(GROUPS + 1):
                for k in range(UNITS):
                    if g < GROUPS:
                        unit(g, k)
                        if ahead and UNITS * g + k + 2 < UNITS * GROUPS:
                            ahead(UNITS * g + k + 2)
                    for st, d in SLOTS[k]:
                        if 0 <= g + d < GROUPS and st in stages:
                            stages[st](g + d)

        block = ctx.enter_context(nc.Block())

        @block.sync
        def _(sp):
            def load_patches(g):
                if g:
                    sp.wait_ge(s["patch_used"], g)
                sp.dma_start(patches[:], xp[g]).then_inc(ld_patch, 16)
            sp.dma_start(cst[:], consts).then_inc(ld_tok, 16)
            sp.dma_start(s96[:], small96).then_inc(ld_tok, 16)
            sp.dma_start(tokw_s[:], tokw).then_inc(ld_tok, 16)
            load_patches(0)
            sp.dma_start(s128[:], small128).then_inc(ld_tok, 16)
            sp.dma_start(win_s[:], w_in).then_inc(ld_mix, 16)
            sp.dma_start(wmin_s[:], w_min).then_inc(ld_mix, 16)
            sp.dma_start(wxp_s[:], w_xp).then_inc(ld_mix, 16)
            sp.dma_start(wdt_s[3 * BCR:XPO, :], w_dt).then_inc(ld_mix, 16)
            sp.dma_start(sel_s[:], sel).then_inc(ld_mix, 16)
            sp.dma_start(wout_s, w_out).then_inc(ld_out, 16)
            sp.dma_start(wbmo_s, w_bmo).then_inc(ld_out, 16)
            sp.dma_start(w1_s[:], w1).then_inc(ld_ffn, 16)
            sp.dma_start(w2_s[:], w2).then_inc(ld_ffn, 16)
            for g in range(1, GROUPS):
                load_patches(g)
            for g in range(GROUPS):
                sp.wait_ge(s["res_made"], g + 1)
                sp.dma_start(out[g], res[:]).then_inc(s["out_done"], 16)
            sp.wait_ge(s["out_done"], 16 * GROUPS)
        LD_TOK, LD_MIX = 64, 80

        @block.tensor
        def _(pe):
            mm = nc.tensor.matmul

            def f_tile(g, i):
                if f_before(g, i):
                    pe.wait_ge(fr_free[i % 3], f_before(g, i))
                return FR[i % 3]

            def b_tile(g, i):
                if b_before(g, i):
                    pe.wait_ge(br_free[i % 2], b_before(g, i))
                return BR[i % 2]

            def centre(P, src):
                for m in range(2):
                    for k in range(2):
                        w = cst[0:HALF, (K_CD if k == m else K_CO):][:, 0:HALF]
                        last = mm(P[0:HALF, m * TOK:(m + 1) * TOK], lhsT=w, rhs=src[:, k], start=(k == 0), stop=(k == 1))
                return last

            def variance(P, sq):
                for k in range(2):
                    last = mm(P[0:HALF, 0:TOK], lhsT=cst[0:HALF, K_J:K_J + HALF], rhs=sq[:, k], start=(k == 0), stop=(k == 1))
                return last

            def f_tok(g):
                P = f_tile(g, T_H)
                if g == 0:
                    pe.wait_ge(ld_tok, LD_TOK)
                    pe.wait_ge(s["posf_made"], 1)
                pe.wait_ge(ld_patch, 16 * (g + 1))
                for m in range(2):
                    T = P[0:HALF, m * TOK:(m + 1) * TOK].rearrange("p (b l) -> p b l", b=GROUP)
                    mm(T, lhsT=cst[0:HALF, 0:HALF], rhs=posf[:, m:m + 1, :].broadcast_to([HALF, GROUP, LEN]), start=True, stop=False)
                    for k in range(PK):
                        last = mm(T[:, :, 2:LEN], lhsT=tokw_s[:, k, m * HALF:(m + 1) * HALF],
                                  rhs=patches[:, k].rearrange("p (b l) -> p b l", b=GROUP), start=False, stop=(k == PK - 1))
                last.then_inc(fr_full[T_H % 3], 1)
                pe.wait_ge(s["h0_made"], g + 1)
                centre(f_tile(g, T_C1), h0[:, g % 2]).then_inc(fr_full[T_C1 % 3], 1)
                pe.wait_ge(s["xc1_made"], g + 1)
                variance(f_tile(g, T_V1), sq1).then_inc(fr_full[T_V1 % 3], 1)

            def f_in(g):
                if g == 0:
                    pe.wait_ge(ld_mix, LD_MIX)
                pe.wait_ge(s["xin_made"], g + 1)
                for d in range(2):
                    P = f_tile(g, T_XF + d)
                    for m in range(2):
                        for k in range(2):
                            last = mm(P[0:HALF, m * TOK:(m + 1) * TOK], lhsT=win_s[:, k, d * DIM + m * HALF:][:, 0:HALF],
                                      rhs=xin[:, g % 2, k], start=(k == 0), stop=(k == 1))
                    last.then_inc(fr_full[(T_XF + d) % 3], 1)

            def proj_in(g, tile, row):
                P = f_tile(g, tile)
                for k in range(2):
                    last = mm(P[:, 0:STOK], lhsT=wmin_s[:, k, row * 128:(row + 1) * 128],
                              rhs=xfb[:, k].rearrange("p d b l -> p (d b l)"), start=(k == 0), stop=(k == 1))
                last.then_inc(fr_full[tile % 3], 1)

            def f_xc(g):
                pe.wait_ge(s["xfb_made"], 4 * (g + 1))
                for c in range(CHUNKS):
                    proj_in(g, T_XC + c, c)

            def f_conv(g):
                if g == 0:
                    fuse_out()
                    pe.wait_ge(s["consts_made"], 1)
                for c in range(CHUNKS):
                    pe.wait_ge(s["xpad_made"], CHUNKS * g + c + 1)
                    P = f_tile(g, T_CONV + c)
                    for k in range(TAPS):
                        last = mm(P[:, 0:STOK].rearrange("p (q l) -> p q l", q=SEQS), lhsT=diag[:, c, k],
                                  rhs=xpad[:, c, :, k:k + LEN], start=(k == 0), stop=(k == TAPS - 1))
                    last.then_inc(fr_full[(T_CONV + c) % 3], 1)
                for c in range(CHUNKS):
                    proj_in(g, T_Z + c, CHUNKS + c)

            def f_dt(g):
                pe.wait_ge(s["u_made"], CHUNKS * (g + 1))
                P = f_tile(g, T_XP)
                for c in range(CHUNKS):
                    last = mm(P[0:XPO, 0:STOK], lhsT=wxp_s[:, c], rhs=u[:, g % 2, c], start=(c == 0), stop=(c == CHUNKS - 1))
                last.then_inc(fr_full[T_XP % 3], 1)
                pe.wait_ge(s["bcf_made"], g + 1)
                for c in range(CHUNKS):
                    P = f_tile(g, T_DT + c)
                    mm(P[:, 0:STOK], lhsT=wdt_s[3 * BCR:XPO, c * 128:(c + 1) * 128], rhs=bcf[3 * BCR:XPO],
                       start=True, stop=True).then_inc(fr_full[(T_DT + c) % 3], 1)

            def bc(g, half):
                pe.wait_ge(s["bc_split"], g + 1)
                for j in range(2 * NH):
                    row = (j // NH) * STATE + half * NH + j % NH
                    i = T_BC + half * 2 * NH + j
                    P = f_tile(g, i)
                    mm(P[:, 0:STOK], lhsT=sel_s[:, row:row + 1].broadcast_to([3 * BCR, 128]), rhs=bc3[:], start=True, stop=True).then_inc(fr_full[i % 3], 1)

            def unit(g, k):
                half, c = k // CHUNKS, k % CHUNKS
                ug = UNITS * g + k
                if ug == 0:
                    pe.wait_ge(s["wf_made"], 1)
                if half == 0 and g:
                    pe.wait_ge(s["yT_copied"], CHUNKS * (g - 1) + c + 1)
                pe.wait_ge(s["p_made"], ug + 1)
                for b in (0, 2, 1):
                    t0, n = BLOCKS[b]
                    for j in range(NH):
                        last = nc.tensor.matmul(YT[c][0:n, b], lhsT=hb[:, ug % HB, j, t0:t0 + n], rhs=ident,
                                                start=(half == 0 and b == 0 and j == 0),
                                                stop=(half == 1 and b == 1 and j == NH - 1), is_transpose=True)
                last.then_inc(s["yT_full"], 1)

            def y_back(g, c):
                pe.wait_ge(s["yT_copied"], CHUNKS * g + c + 1)
                P = b_tile(g, T_Y + c)
                for b, (t0, n) in enumerate(BLOCKS):
                    last = nc.tensor.transpose(P[:, t0:t0 + n], yTs[0:n, b], cst[0:n, K_ID:K_ID + n])
                last.then_inc(br_full[(T_Y + c) % 2], 1)
                last_turned = CHUNKS * g + c + 1
                return last_turned

            def fuse_out():
                pe.wait_ge(ld_out, 32)
                for c in range(CHUNKS):
                    for k in range(2):
                        last = mm(YT[c][:, :, :].rearrange("p a b -> p (a b)")[:, 0:DIM], lhsT=wout_s[:, k, c * 128:(c + 1) * 128],
                                  rhs=wbmo_s[:, k], start=(k == 0), stop=(k == 1))
                last.then_inc(s["wf_full"], 1)

            def b_mo(g):
                pe.wait_ge(s["ys_made"], CHUNKS * (g + 1))
                P = b_tile(g, T_MO)
                for m in range(2):
                    for c in range(CHUNKS):
                        last = mm(P[0:HALF, m * TOK:(m + 1) * TOK], lhsT=wf[:, c, m * HALF:(m + 1) * HALF], rhs=ys[:, c],
                                  start=(c == 0), stop=(c == CHUNKS - 1))
                last.then_inc(br_full[T_MO % 2], 1)

            def b_ln(g):
                pe.wait_ge(s["h1_made"], g + 1)
                centre(b_tile(g, T_C2), h1).then_inc(br_full[T_C2 % 2], 1)
                pe.wait_ge(s["xc2_made"], 2 * g + 1)
                variance(b_tile(g, T_V2), sq2).then_inc(br_full[T_V2 % 2], 1)

            def b_ln2(g):
                pe.wait_ge(s["h2_made"], g + 1)
                centre(b_tile(g, T_C3), h2).then_inc(br_full[T_C3 % 2], 1)
                pe.wait_ge(s["xc2_made"], 2 * g + 2)
                variance(b_tile(g, T_V3), sq2).then_inc(br_full[T_V3 % 2], 1)

            def b_gate(g):
                pe.wait_ge(s["tmw_made"], g + 1)
                P = b_tile(g, T_G)
                for k in range(2):
                    last = mm(P[:, 0:GROUP * EXPERTS], lhsT=cst[0:HALF, K_ONE:K_ONE + 128],
                              rhs=tmw[:, k].rearrange("p b e -> p (b e)"), start=(k == 0), stop=(k == 1))
                last.then_inc(br_full[T_G % 2], 1)

            def b_up(g):
                if g == 0:
                    pe.wait_ge(ld_ffn, 32)
                pe.wait_ge(s["t2_made"], g + 1)
                for i in range(FT // 3):
                    P = b_tile(g, T_UP + i)
                    for j in range(3):
                        for k in range(2):
                            last = mm(P[:, j * TOK:(j + 1) * TOK], lhsT=w1_s[:, k, (3 * i + j) * 128:(3 * i + j + 1) * 128],
                                      rhs=t2[:, k], start=(k == 0), stop=(k == 1))
                    last.then_inc(br_full[(T_UP + i) % 2], 1)

            def b_out(g):
                P = b_tile(g, T_O)
                for e in range(EXPERTS):
                    pe.wait_ge(s["hid_made"], EXPERTS * g + e + 1)
                    for f in range(e * FPE, (e + 1) * FPE):
                        for m in range(2):
                            last = mm(P[0:HALF, m * TOK:(m + 1) * TOK], lhsT=w2_s[:, f, m * HALF:(m + 1) * HALF], rhs=hid[:, f],
                                      start=(f == 0 and m == 0), stop=(f == FT - 1), skip_group_check=True)
                last.then_inc(br_full[T_O % 2], 1)

            program(unit, {"f_tok": f_tok, "f_in": f_in, "f_xc": f_xc, "f_conv": f_conv, "f_dt": f_dt,
                           "bc0": lambda g: bc(g, 0), "bc1": lambda g: bc(g, 1),
                           "y0": lambda g: y_back(g, 0), "y1": lambda g: y_back(g, 1), "y2": lambda g: y_back(g, 2),
                           "b_mo": b_mo, "b_ln": b_ln, "b_ln2": b_ln2, "b_gate": b_gate, "b_up": b_up, "b_out": b_out})

        @block.scalar
        def _(act):
            A = nc.scalar.activation

            def f_full(g, i):
                act.wait_ge(fr_full[i % 3], f_before(g, i) + 1)
                return FR[i % 3]

            def b_full(g, i):
                act.wait_ge(br_full[i % 2], b_before(g, i) + 1)
                return BR[i % 2]

            act.wait_ge(ld_tok, LD_TOK)
            act.wait_ge(s["posf_made"], 1)
            A(Aneg[:], s128[:, C_ALOG:C_ALOG + CHUNKS * STATE], ACT.Exp).then_inc(s["a_log_exp"], 1)

            def f_tok(g):
                P = f_full(g, T_H)
                if g >= 2:
                    act.wait_ge(s["h2_made"], g - 1)
                A(h0[:, g % 2].rearrange("p m t -> p (m t)"), P[0:HALF, 0:2 * TOK], ACT.Copy).then_inc(s["h0_made"], 1)
                act.wait_ge(s["h0_made"], g + 1)
                act.sem_inc(fr_free[T_H % 3], 1)
                P = f_full(g, T_C1)
                if g:
                    act.wait_ge(s["xin_made"], g)
                A(xc1[:].rearrange("p m t -> p (m t)"), P[0:HALF, 0:2 * TOK], ACT.Copy)
                A(sq1[:].rearrange("p m t -> p (m t)"), P[0:HALF, 0:2 * TOK], ACT.Square).then_inc(s["xc1_made"], 1)
                act.wait_ge(s["xc1_made"], g + 1)
                act.sem_inc(fr_free[T_C1 % 3], 1)
                P = f_full(g, T_V1)
                A(rs1[:, 0], P[0:HALF, 0:TOK], ACT.Ln, bias=eps[0:HALF, :]).then_inc(s["rln1"], 1)
                act.wait_ge(s["rln1"], g + 1)
                act.sem_inc(fr_free[T_V1 % 3], 1)
                A(rs1[:, 1], rs1[:, 0], ACT.Exp, scale=-0.5).then_inc(s["rs1_made"], 1)

            def f_in(g):
                for d in range(2):
                    P = f_full(g, T_XF + d)
                    for m in range(2):
                        src = P[0:HALF, m * TOK:(m + 1) * TOK].rearrange("p (b l) -> p b l", b=GROUP)
                        dst = xfb[:, m, d] if d == 0 else xfb[:, m, d, :, ::-1]
                        last = A(dst, src, ACT.Identity, bias=s96[:, S_INB + 2 * d + m:][:, 0:1]).then_inc(s["xfb_made"], 1)
                    act.wait_ge(s["xfb_made"], 4 * g + 2 * d + 2)
                    act.sem_inc(fr_free[(T_XF + d) % 3], 1)

            def f_xc(g):
                if g == 0:
                    act.wait_ge(s["pads_made"], 1)
                for c in range(CHUNKS):
                    P = f_full(g, T_XC + c)
                    A(xpad[:, c, :, TAPS - 1:], P[:, 0:STOK].rearrange("p (q l) -> p q l", q=SEQS), ACT.Copy)\
                        .then_inc(s["xpad_made"], 1)
                    act.wait_ge(s["xpad_made"], CHUNKS * g + c + 1)
                    act.sem_inc(fr_free[(T_XC + c) % 3], 1)

            def f_conv(g):
                for c in range(CHUNKS):
                    P = f_full(g, T_CONV + c)
                    if g >= 2:
                        act.wait_ge(s["y_skip"], CHUNKS * (g - 2) + c + 1)
                    A(u[:, g % 2, c], P[:, 0:STOK], ACT.Silu, bias=s128[:, C_CB + c:C_CB + c + 1]).then_inc(s["u_made"], 1)
                    act.wait_ge(s["u_made"], CHUNKS * g + c + 1)
                    act.sem_inc(fr_free[(T_CONV + c) % 3], 1)
                for c in range(CHUNKS):
                    P = f_full(g, T_Z + c)
                    if g >= 2:
                        act.wait_ge(s["y_gated"], CHUNKS * (g - 2) + c + 1)
                    A(sz[:, g % 2, c], P[:, 0:STOK], ACT.Silu).then_inc(s["sz_made"], 1)
                    act.wait_ge(s["sz_made"], CHUNKS * g + c + 1)
                    act.sem_inc(fr_free[(T_Z + c) % 3], 1)

            def f_dt(g):
                P = f_full(g, T_XP)
                if g:
                    act.wait_ge(fr_full[(T_BC + BCR - 1) % 3], f_before(g - 1, T_BC + BCR - 1) + 1)
                A(bc3[:], P[0:3 * BCR, 0:STOK], ACT.Copy)
                A(bcf[:], P[0:XPO, 0:STOK], ACT.Copy).then_inc(s["bcf_made"], 1)
                act.wait_ge(s["bcf_made"], g + 1)
                act.sem_inc(fr_free[T_XP % 3], 1)
                if g >= 3:
                    act.wait_ge(br_full[T_O % 2], b_before(g - 3, T_O) + 1)
                if g == 0:
                    act.wait_ge(s["wf_full"], 1)
                for c in range(CHUNKS):
                    P = f_full(g, T_DT + c)
                    bias = s128[:, C_DTB + c:C_DTB + c + 1]
                    A(spe[:, c], P[:, 0:STOK], ACT.Abs, bias=bias)
                    A(dt[:, c], P[:, 0:STOK], ACT.Relu, bias=bias).then_inc(s["sp_abs"], 1)
                    act.wait_ge(s["sp_abs"], CHUNKS * g + c + 1)
                    act.sem_inc(fr_free[(T_DT + c) % 3], 1)
                A(spe, spe, ACT.Exp, scale=-1.0).then_inc(s["sp_exp"], 1)
                act.wait_ge(s["sp_exp"], g + 1)
                A(spl, spe, ACT.Ln, bias=1.0).then_inc(s["sp_log"], 1)
                act.wait_ge(s["sp_log"], g + 1)
                A(spi, spl, ACT.Exp, scale=-1.0).then_inc(s["sp_parts"], 1)

            def bc(g, half):
                if g:
                    act.wait_ge(s["p_made"], UNITS * (g - 1) + CHUNKS * (half + 1))
                for j in range(2 * NH):
                    i = T_BC + half * 2 * NH + j
                    P = f_full(g, i)
                    A(BC[:, half, j], P[:, 0:STOK], ACT.Copy).then_inc(fr_free[i % 3], 1)
                    if j == 2 * NH - 1:
                        act.wait_ge(fr_free[i % 3], f_before(g, i) + 1)
                        act.sem_inc(s["B_made"], 1)

            def ahead(ug):
                g, k = ug // UNITS, ug % UNITS
                half, c = k // CHUNKS, k % CHUNKS
                if ug == 0:
                    act.wait_ge(s["a_made"], 1)
                if k == 0:
                    act.wait_ge(s["dt_made"], g + 1)
                if ug >= AB:
                    act.wait_ge(s["h_made"], ug - AB + 1)
                for j in range(NH):
                    n = c * STATE + half * NH + j
                    last = A(a[:, ug % AB, j, :, 1:LEN], dt[:, c].rearrange("p (q l) -> p q l", q=SEQS)[:, :, 1:LEN],
                             ACT.Exp, scale=Aneg[:, n:n + 1])
                last.then_inc(s["a_ready"], 1)

            def y_copy(g, c):
                act.wait_ge(s["yT_full"], UNITS * g + CHUNKS + c + 1)
                if CHUNKS * g + c:
                    n = CHUNKS * g + c - 1
                    act.wait_ge(br_full[n % CHUNKS % 2], b_before(n // CHUNKS, T_Y + n % CHUNKS) + 1)
                A(yTs[0:BLOCKS[0][1], 0:2], YT[c][0:BLOCKS[0][1], 0:2], ACT.Copy)
                A(yTs[0:BLOCKS[2][1], 2], YT[c][0:BLOCKS[2][1], 2], ACT.Copy).then_inc(s["yT_copied"], 1)

            def b_mo(g):
                P = b_full(g, T_MO)
                for m in range(2):
                    A(h1[:, m], P[0:HALF, m * TOK:(m + 1) * TOK], ACT.Identity, bias=s96[:, S_OUTB + m:][:, 0:1])\
                        .then_inc(s["mo_made"], 1)
                act.wait_ge(s["mo_made"], 2 * (g + 1))
                act.sem_inc(br_free[T_MO % 2], 1)

            def norm(g, which, tc, tv):
                P = b_full(g, tc)
                n = 2 * g + which
                if n:
                    act.wait_ge(s["t2_made" if which == 0 else "h2_made"], g if which == 0 else g + 1)
                A(xc2[:].rearrange("p m t -> p (m t)"), P[0:HALF, 0:2 * TOK], ACT.Copy)
                A(sq2[:].rearrange("p m t -> p (m t)"), P[0:HALF, 0:2 * TOK], ACT.Square).then_inc(s["xc2_made"], 1)
                act.wait_ge(s["xc2_made"], n + 1)
                act.sem_inc(br_free[tc % 2], 1)
                P = b_full(g, tv)
                A(rs2[:, 0], P[0:HALF, 0:TOK], ACT.Ln, bias=eps[0:HALF, :]).then_inc(s["rln2"], 1)
                act.wait_ge(s["rln2"], n + 1)
                act.sem_inc(br_free[tv % 2], 1)
                A(rs2[:, 1], rs2[:, 0], ACT.Exp, scale=-0.5).then_inc(s["rs2_made"], 1)

            def b_gate(g):
                act.wait_ge(s["gate_in"], g + 1)
                A(ge_[:], gl[:], ACT.Exp).then_inc(s["gate_exp"], 1)

            def b_up(g):
                if g:
                    act.wait_ge(br_full[T_O % 2], b_before(g - 1, T_O) + 1)
                for i in range(FT // 3):
                    P = b_full(g, T_UP + i)
                    for j in range(3):
                        f = 3 * i + j
                        A(hid[:, f], P[:, j * TOK:(j + 1) * TOK], ACT.Gelu, bias=s128[:, C_B1 + f:C_B1 + f + 1])\
                            .then_inc(s["hid_raw"], 1)
                    act.wait_ge(s["hid_raw"], FT * g + 3 * i + 3)
                    act.sem_inc(br_free[(T_UP + i) % 2], 1)

            program(lambda g, k: None,
                    {"f_tok": f_tok, "f_in": f_in, "f_xc": f_xc, "f_conv": f_conv, "f_dt": f_dt,
                     "bc0": lambda g: bc(g, 0), "bc1": lambda g: bc(g, 1),
                     "y0": lambda g: y_copy(g, 0), "y1": lambda g: y_copy(g, 1), "y2": lambda g: y_copy(g, 2),
                     "b_mo": b_mo, "b_ln": lambda g: norm(g, 0, T_C2, T_V2), "b_ln2": lambda g: norm(g, 1, T_C3, T_V3),
                     "b_gate": b_gate, "b_up": b_up}, ahead)

        @block.vector
        def _(dve):
            V = nc.vector
            chain = [0]

            def then(ins):
                chain[0] += 1
                ins.then_inc(s["dve_chain"], 1)
                dve.wait_ge(s["dve_chain"], chain[0])

            V.memset(eps[:], LN_EPS)
            dve.wait_ge(ld_tok, LD_TOK)
            V.tensor_copy(posf[:, :, 0:1], s96[:, S_CLS:S_CLS + 2].rearrange("p (m o) -> p m o", o=1))
            pos = s96[:, S_POS:S_POS + 74].rearrange("p (m l) -> p m l", m=2)
            V.tensor_tensor(posf[:, :, 1:2], pos[:, :, 0:1], s96[:, S_CT:S_CT + 2].rearrange("p (m o) -> p m o", o=1), ALU.add)
            V.tensor_tensor(posf[:, :, 2:LEN], pos[:, :, 1:37],
                            s96[:, S_TOKB:S_TOKB + 2].rearrange("p (m o) -> p m o", o=1).broadcast_to([HALF, 2, PATCHES]),
                            ALU.add).then_inc(s["posf_made"], 1)
            V.memset(xpad[:, :, :, 0:TAPS - 1], 0.0).then_inc(s["pads_made"], 1)
            dve.wait_ge(s["a_log_exp"], 1)
            V.tensor_scalar(Aneg[:], Aneg[:], -1.0, None, ALU.mult).then_inc(s["a_made"], 1)
            for c in range(CHUNKS):
                for k in range(TAPS):
                    last = V.tensor_scalar(diag[:, c, k], ident, s128[:, C_CW + TAPS * c + k:][:, 0:1], None, ALU.mult)
            last.then_inc(s["consts_made"], 1)
            for i in range(AB):
                last = V.memset(a[:, i, :, :, 0:1], 0.0)
            then(last)
            dve.wait_ge(s["wf_full"], 1)
            for c in range(CHUNKS):
                last = V.tensor_copy(wf[:, c], YT[c][:, :, :].rearrange("p a b -> p (a b)")[:, 0:DIM])
            last.then_inc(s["wf_made"], 1)

            def unit(g, k):
                half, c = k // CHUNKS, k % CHUNKS
                ug = UNITS * g + k
                dve.wait_ge(s["B_made"], 2 * g + half + 1)
                if half == 0:
                    dve.wait_ge(s["du_made"], CHUNKS * g + c + 1)
                if ug >= HB:
                    dve.wait_ge(s["yT_full"], ug - HB + 1)
                H = hb[:, ug % HB]
                V.tensor_tensor(H, du[:, c:c + 1].broadcast_to([128, NH, STOK]), BC[:, half, 0:NH], ALU.mult)\
                    .then_inc(s["b_made"], 1)
                dve.wait_ge(s["b_made"], ug + 1)
                dve.wait_ge(s["a_ready"], ug + 1)
                flat = H.rearrange("p n t -> p (n t)")
                V.tensor_tensor_scan(flat, a[:, ug % AB].rearrange("p n q l -> p (n q l)"), flat, 0.0, ALU.mult, ALU.add)\
                    .then_inc(s["h_made"], 1)
                dve.wait_ge(s["h_made"], ug + 1)
                V.tensor_tensor(H, H, BC[:, half, NH:2 * NH], ALU.mult).then_inc(s["p_made"], 1)

            def y_finish(g, c):
                n = CHUNKS * g + c
                dve.wait_ge(br_full[(T_Y + c) % 2], b_before(g, T_Y + c) + 1)
                V.scalar_tensor_tensor(yg[:], u[:, g % 2, c], s128[:, C_D + c:C_D + c + 1], BR[(T_Y + c) % 2][:, 0:STOK],
                                       ALU.mult, ALU.add).then_inc(s["y_skip"], 1)
                dve.wait_ge(s["y_skip"], n + 1)
                dve.sem_inc(br_free[(T_Y + c) % 2], 1)
                dve.wait_ge(s["sz_made"], n + 1)
                V.tensor_tensor(yg[:], yg[:], sz[:, g % 2, c], ALU.mult).then_inc(s["y_gated"], 1)
                dve.wait_ge(s["y_gated"], n + 1)
                if g:
                    dve.wait_ge(br_full[T_MO % 2], b_before(g - 1, T_MO) + 1)
                y4 = yg[:].rearrange("p (d b l) -> p d b l", d=2, b=GROUP)
                V.tensor_tensor(ys[:, c].rearrange("p (b l) -> p b l", b=GROUP), y4[:, 0], y4[:, 1, :, ::-1], ALU.add)\
                    .then_inc(s["ys_made"], 1)
                dve.wait_ge(s["ys_made"], n + 1)

            def b_gate(g):
                dve.wait_ge(s["t2_made"], g + 1)
                then(V.reduce_sum(tm[:], t2[:].rearrange("p m (b l) -> p m b l", b=GROUP), AX.X))
                wgt = s96[:, S_WG:S_WG + 6].rearrange("p (m o e) -> p m o e", m=2, o=1)
                for m in range(2):
                    last = V.tensor_tensor(tmw[:, m], tm[:, m].rearrange("p (b o) -> p b o", o=1).broadcast_to([HALF, GROUP, EXPERTS]),
                                           wgt[:, m].broadcast_to([HALF, GROUP, EXPERTS]), ALU.mult)
                last.then_inc(s["tmw_made"], 1)
                dve.wait_ge(br_full[T_G % 2], b_before(g, T_G) + 1)
                P = BR[T_G % 2][:, 0:GROUP * EXPERTS].rearrange("p (b e) -> p b e", b=GROUP)
                then(V.tensor_scalar(gl[:], P, 1.0 / LEN, None, ALU.mult))
                dve.sem_inc(br_free[T_G % 2], 1)
                bcast = lambda col: gm[:, :, col:col + 1].broadcast_to([128, GROUP, EXPERTS])
                then(V.reduce_max(gm[:, :, 0:1], gl[:], AX.X))
                V.tensor_tensor(gl[:], gl[:], bcast(0), ALU.subtract).then_inc(s["gate_in"], 1)
                dve.wait_ge(s["gate_exp"], g + 1)
                then(V.reduce_sum(gm[:, :, 1:2], ge_[:], AX.X))
                then(V.reciprocal(gm[:, :, 2:3], gm[:, :, 1:2]))
                then(V.tensor_tensor(ge_[:], ge_[:], bcast(2), ALU.mult))
                then(V.reduce_max(gm[:, :, 3:4], ge_[:], AX.X))
                then(V.tensor_tensor(gl[:], ge_[:], bcast(3), ALU.is_equal))
                then(V.tensor_scalar(gm[:, :, 0:1], gl[:, :, 0:1], -1.0, 1.0, ALU.mult, ALU.add))
                then(V.tensor_tensor(gl[:, :, 1:2], gl[:, :, 1:2], gm[:, :, 0:1], ALU.mult))
                then(V.tensor_tensor(gm[:, :, 1:2], gm[:, :, 0:1], gl[:, :, 1:2], ALU.subtract))
                then(V.tensor_tensor(gl[:, :, 2:3], gl[:, :, 2:3], gm[:, :, 1:2], ALU.mult))
                if g:
                    dve.wait_ge(s["hid_made"], EXPERTS * g)
                V.tensor_tensor(wg[:], ge_[:], gl[:], ALU.mult).then_inc(s["w_made"], 1)
                dve.wait_ge(s["w_made"], g + 1)
                b2 = s96[:, S_B2:S_B2 + 6].rearrange("p (m o e) -> p m o e", m=2, o=1)
                for m in range(2):
                    last = V.tensor_tensor(b2w[:, m], b2[:, m].broadcast_to([HALF, GROUP, EXPERTS]), wg[0:HALF], ALU.mult)
                then(last)
                then(V.reduce_sum(b2s[:], b2w[:], AX.X))
                for m in range(2):
                    H = h2[:, m].rearrange("p (b l) -> p b l", b=GROUP)
                    last = V.tensor_tensor(H, H, b2s[:, m].rearrange("p (b o) -> p b o", o=1).broadcast_to([HALF, GROUP, LEN]), ALU.add)
                last.then_inc(s["h2b_made"], 1)

            def b_out(g):
                dve.wait_ge(br_full[T_O % 2], b_before(g, T_O) + 1)
                dve.wait_ge(s["h2b_made"], g + 1)
                V.tensor_tensor(res[:].rearrange("p m t -> p (m t)"), h2[:].rearrange("p m t -> p (m t)"),
                                BR[T_O % 2][0:HALF, 0:2 * TOK], ALU.add).then_inc(s["res_made"], 1)
                dve.wait_ge(s["res_made"], g + 1)
                dve.sem_inc(br_free[T_O % 2], 1)

            program(unit, {"y0": lambda g: y_finish(g, 0), "y1": lambda g: y_finish(g, 1), "y2": lambda g: y_finish(g, 2),
                           "b_gate": b_gate, "b_out": b_out})

        @block.gpsimd
        def _(pool):
            G = nc.gpsimd
            chain = [0]

            def then(ins):
                chain[0] += 1
                ins.then_inc(s["pool_chain"], 1)
                pool.wait_ge(s["pool_chain"], chain[0])

            def normed(out_, xc, rs):
                for m in range(2):
                    last = G.tensor_tensor(out_[:, m], xc[:, m], rs[:, 1], ALU.mult)
                return last

            def f_tok(g):
                pool.wait_ge(s["rs1_made"], g + 1)
                if g >= 2:
                    pool.wait_ge(s["h1_made"], g - 1)
                normed(xin[:, g % 2], xc1, rs1).then_inc(s["xin_made"], 1)

            def f_in(g):
                pool.wait_ge(s["h0_made"], g + 1)
                pool.sem_inc(s["patch_used"], 1)

            def f_dt(g):
                pool.wait_ge(s["bcf_made"], g + 1)
                bcr = bcf[0:3 * BCR]
                then(G.tensor_tensor(bcr, bcr, bc3[:], ALU.subtract))
                then(G.tensor_copy(bc3[BCR:2 * BCR], bcr[BCR:2 * BCR]))
                then(G.tensor_copy(bcm[2 * BCR:3 * BCR], bcr[2 * BCR:3 * BCR]))
                G.tensor_tensor(bc3[2 * BCR:3 * BCR], bcr[2 * BCR:3 * BCR], bcm[2 * BCR:3 * BCR], ALU.subtract)\
                    .then_inc(s["bc_split"], 1)
                pool.wait_ge(s["bc_split"], g + 1)
                pool.wait_ge(s["sp_parts"], g + 1)
                D = dt[:]
                then(G.tensor_tensor(D, D, spl, ALU.add))
                then(G.tensor_scalar(spl, spe, 1.0, -1.0, ALU.add, ALU.add))
                then(G.tensor_tensor(spe, spe, spl, ALU.subtract))
                then(G.tensor_tensor(spe, spe, spi, ALU.mult))
                G.tensor_tensor(D, D, spe, ALU.add).then_inc(s["dt_made"], 1)

            def f_du(g, c):
                if c == 0:
                    pool.wait_ge(s["dt_made"], g + 1)
                pool.wait_ge(s["u_made"], CHUNKS * g + c + 1)
                if g:
                    pool.wait_ge(s["b_made"], UNITS * (g - 1) + CHUNKS + c + 1)
                G.tensor_tensor(du[:, c], dt[:, c], u[:, g % 2, c], ALU.mult).then_inc(s["du_made"], 1)

            def b_mo(g):
                pool.wait_ge(s["mo_made"], 2 * (g + 1))
                G.tensor_tensor(h1[:], h1[:], xin[:, g % 2], ALU.add).then_inc(s["h1_made"], 1)

            def b_ln(g):
                pool.wait_ge(s["rs2_made"], 2 * g + 1)
                then(normed(xc2, xc2, rs2))
                for m in range(2):
                    last = G.tensor_scalar(xc2[:, m], xc2[:, m], s96[:, S_LNG + m:][:, 0:1], s96[:, S_LNB + m:][:, 0:1],
                                           ALU.mult, ALU.add)
                then(last)
                if g:
                    pool.wait_ge(s["res_made"], g)
                G.tensor_tensor(h2[:], xc2[:], h0[:, g % 2], ALU.add).then_inc(s["h2_made"], 1)

            def b_ln2(g):
                pool.wait_ge(s["rs2_made"], 2 * g + 2)
                if g:
                    pool.wait_ge(s["out_done"], 16 * g)
                normed(t2, xc2, rs2).then_inc(s["t2_made"], 1)

            def b_up(g):
                pool.wait_ge(s["w_made"], g + 1)
                for e in range(EXPERTS):
                    pool.wait_ge(s["hid_raw"], FT * g + FPE * (e + 1))
                    for b in range(GROUP):
                        X = hid[:, e * FPE:(e + 1) * FPE, b * LEN:(b + 1) * LEN]
                        last = G.tensor_scalar(X, X, wg[:, b, e:e + 1], None, ALU.mult)
                    last.then_inc(s["hid_made"], 1)

            program(lambda g, k: None, {"f_tok": f_tok, "f_in": f_in, "f_dt": f_dt, "b_mo": b_mo, "b_ln": b_ln,
                                        "b_ln2": b_ln2, "b_up": b_up,
                                        "du0": lambda g: f_du(g, 0), "du1": lambda g: f_du(g, 1),
                                        "du2": lambda g: f_du(g, 2)})


def kernel(**inputs):
    import ml_dtypes
    import numpy as np
    import concourse.bacc as bacc
    from concourse import mybir as _mybir
    from concourse.bass_utils import run_bass_kernel_spmd as run

    I = {k: np.asarray(v) for k, v in inputs.items()}
    f = lambda k: I[k]
    cc = np.ascontiguousarray

    def rows(w, p):
        return cc(w.reshape(w.shape[0] // p, p, -1).transpose(1, 0, 2))

    side = 96 // 16
    x = f("x").reshape(GROUPS, GROUP, 3, side, 16, side, 16).transpose(0, 2, 4, 6, 1, 3, 5)
    x = x.reshape(GROUPS, PK, 128, GROUP * PATCHES).transpose(0, 2, 1, 3)
    col = lambda v: rows(v.reshape(-1, 1), HALF)[:, :, 0]
    small96 = np.concatenate([
        rows(f("L0_tok_pos_embedding")[0].T, HALF).reshape(HALF, -1), col(f("L0_tok_b")), col(f("cls_tok")),
        col(f("L0_tok_class_token")), col(f("L0_attn_bm_in_b")), col(f("L0_attn_bm_out_b")), col(f("L0_attn_ln_g")),
        col(f("L0_attn_ln_b")), rows(f("L0_ffn_Wg").T, HALF).reshape(HALF, -1),
        rows(f("L0_ffn_b2").T, HALF).reshape(HALF, -1)], axis=1)
    ch = lambda v: rows(v.reshape(v.shape[0], -1), 128).reshape(128, -1)
    small128 = np.concatenate([
        ch(f("L0_attn_m_conv_w")), ch(f("L0_attn_m_conv_b")), ch(f("L0_attn_m_dt_b")), ch(f("L0_attn_m_A_log")),
        ch(f("L0_attn_m_D")), ch(f("L0_ffn_b1").reshape(-1))], axis=1)
    eye = np.eye(128, dtype=np.float32)
    consts = np.zeros((128, K_END), np.float32)
    consts[:, K_ID:K_ID + 128] = eye
    consts[:HALF, K_CD:K_CD + HALF] = eye[:HALF, :HALF] - np.float32(1.0 / DIM)
    consts[:HALF, K_CO:K_CO + HALF] = -np.float32(1.0 / DIM)
    consts[:HALF, K_J:K_J + HALF] = np.float32(1.0 / DIM)
    consts[:, K_ONE:K_ONE + 128] = 1.0
    sel = np.zeros((3 * BCR, BCR), ml_dtypes.bfloat16)
    for r in range(3 * BCR):
        sel[r, r % BCR] = 1
    xw = f("L0_attn_m_xproj_w").T
    xw = np.concatenate([xw[:, DT_RANK:]] * 3 + [xw[:, :DT_RANK]], axis=1)
    arrays = {
        "xp": x, "tokw": rows(f("L0_tok_W").T, 128), "small96": small96, "small128": small128, "consts": consts,
        "sel": sel, "w_in": rows(f("L0_attn_bm_in_w").T, HALF), "w_min": rows(f("L0_attn_m_in_w").T, HALF),
        "w_xp": rows(xw, 128), "w_dt": f("L0_attn_m_dt_w").T, "w_out": rows(f("L0_attn_m_out_w"), HALF),
        "w_bmo": rows(f("L0_attn_bm_out_w").T, HALF),
        "w1": rows(f("L0_ffn_W1").transpose(1, 0, 2).reshape(DIM, -1), HALF),
        "w2": rows(f("L0_ffn_W2").reshape(-1, DIM), 128)}
    nc = bacc.Bacc("TRN2", target_bir_lowering=False, num_devices=1)
    arrays = {f"in_{k}": cc(v) for k, v in arrays.items()}
    args = [nc.dram_tensor(k, v.shape, _mybir.dt.from_np(v.dtype), kind="ExternalInput").ap() for k, v in arrays.items()]
    args.append(nc.dram_tensor("out_0", (GROUPS, HALF, 2, TOK), _mybir.dt.float32, kind="ExternalOutput").ap())
    tower(nc, *args)
    r = run(nc, [arrays], core_ids=[0])
    got = r.results[0]["out_0"].reshape(GROUPS, HALF, 2, GROUP, LEN)
    return cc(got.transpose(0, 3, 4, 2, 1).reshape(BATCH, LEN, DIM))
```

```python
import concourse.bass as bass
from concourse import mybir
from contextlib import ExitStack

BATCH, LEN, DIM = 16, 38, 192
HALF = DIM // 2
PATCHES, PATCH_DIM = 36, 768
INNER, STATE, TAPS, DT_RANK = 384, 16, 4, 12
CHUNKS = INNER // 128
EXPERTS, HIDDEN = 3, 768
GROUP = 4
GROUPS = BATCH // GROUP
TOK = GROUP * LEN
SEQS = 2 * GROUP
STOK = SEQS * LEN
PK = PATCH_DIM // 128
NH = STATE // 2
UNITS = 2 * CHUNKS
FT = EXPERTS * HIDDEN // 128
FPE = HIDDEN // 128
BCR = 2 * STATE
BCP = 4
XPO = 3 * BCR + DT_RANK
BLOCKS = [(0, 3 * LEN), (3 * LEN, 3 * LEN), (6 * LEN, 2 * LEN)]
LN_EPS = 1e-5

S_POS, S_TOKB, S_CLS, S_CT, S_INB, S_OUTB, S_LNG, S_LNB, S_WG, S_B2, S_END = 0, 74, 76, 78, 80, 84, 86, 88, 90, 96, 102
C_CW, C_CB, C_DTB, C_ALOG, C_D, C_B1, C_END = 0, 12, 15, 18, 66, 69, 87
K_ID, K_CD, K_CO, K_J, K_ONE, K_END = 0, 128, 224, 320, 416, 544


def tower(nc, xp, tokw, small96, small128, consts, sel, w_in, w_min, w_xp, w_dt, w_out, w_bmo, w1, w2, out):
    f32, bf16 = mybir.dt.float32, mybir.dt.bfloat16
    ALU, ACT, AX = mybir.AluOpType, mybir.ActivationFunctionType, mybir.AxisListType
    with ExitStack() as ctx:
        def sb(name, shape, dt=f32):
            return ctx.enter_context(nc.sbuf_tensor(name, shape, dt))

        def sem(name):
            return ctx.enter_context(nc.semaphore(name))

        tokw_s = sb("tokw_s", [128, PK, DIM])
        s96 = sb("s96", [HALF, S_END])
        s128 = sb("s128", [128, C_END])
        cst = sb("cst", [128, K_END])
        sel_s = sb("sel_s", [3 * BCR, BCR], bf16)
        win_s = sb("win_s", [HALF, 2, 2 * DIM])
        wmin_s = sb("wmin_s", [HALF, 2, 2 * INNER])
        wxp_s = sb("wxp_s", [128, CHUNKS, XPO])
        wdt_s = sb("wdt_s", [128, INNER])
        w1_s = sb("w1_s", [HALF, 2, EXPERTS * HIDDEN])
        w2_s = sb("w2_s", [128, FT, DIM])
        ident = cst[:, K_ID:K_ID + 128]
        posf = sb("posf", [HALF, 2, LEN])
        eps = sb("eps", [128, 1])
        Aneg = sb("Aneg", [128, CHUNKS * STATE])
        wf = sb("wf", [128, CHUNKS, DIM])
        patches = sb("patches", [128, PK, GROUP * PATCHES])
        h0 = sb("h0", [HALF, 3, 2, TOK])
        xc1 = sb("xc1", [HALF, 2, TOK])
        sq1 = sb("sq1", [HALF, 2, TOK])
        rs1 = sq1
        xin = sb("xin", [HALF, 2, 2, TOK])
        xfb = sb("xfb", [HALF, 2, 2, GROUP, LEN])
        xpad = sb("xpad", [128, CHUNKS, SEQS, LEN + TAPS - 1])
        conv = sb("conv", [128, CHUNKS, STOK])
        spw = conv
        u = sb("u", [128, 2, CHUNKS, STOK])
        sz = sb("sz", [128, 2, CHUNKS, STOK])
        dt = sb("dt", [128, CHUNKS, STOK])
        du = sb("du", [128, CHUNKS, STOK])
        shared = sb("shared", [128, FT * TOK])
        hid = shared[:].rearrange("p (f t) -> p f t", f=FT)
        sp3 = shared[:].rearrange("p (k c t) -> p k c t", k=3, c=CHUNKS)
        spe, spl, spi = sp3[:, 0], sp3[:, 1], sp3[:, 2]
        wout_s = shared[0:HALF, 0:2 * INNER].rearrange("p (k n) -> p k n", k=2)
        wbmo_s = shared[0:HALF, 2 * INNER:2 * INNER + 2 * DIM].rearrange("p (k n) -> p k n", k=2)
        bcf = sb("bcf", [XPO, STOK])
        bc3 = sb("bc3", [3 * BCR, STOK], bf16)
        bcm = sb("bcm", [3 * BCR, STOK], bf16)
        BC = sb("BC", [128, 2, 2 * NH, STOK])
        AB = 3
        a = sb("a", [128, AB, NH, SEQS, LEN])
        HB = 2
        hb = sb("hb", [128, HB, NH, STOK])
        yTs = sb("yTs", [128, 3, 128])
        yg = sb("yg", [128, STOK])
        ys = sb("ys", [128, CHUNKS, TOK])
        h1 = sb("h1", [HALF, 2, TOK])
        xc2 = h1
        sq2 = sb("sq2", [HALF, 2, TOK])
        rs2 = sq2
        h2 = sb("h2", [HALF, 2, TOK])
        t2 = sb("t2", [HALF, 2, TOK])
        tm = sb("tm", [HALF, 2, GROUP])
        tmw = sb("tmw", [HALF, 2, GROUP, EXPERTS])
        gl = sb("gl", [128, GROUP, EXPERTS])
        gm = sb("gm", [128, GROUP, 4])
        ge_ = sb("ge_", [128, GROUP, EXPERTS])
        wg = sb("wg", [128, GROUP, EXPERTS])
        res = t2

        BANKS = 5
        PS = [ctx.enter_context(nc.psum_tensor(f"PS{i}", [128, 512], f32)) for i in range(BANKS)]
        YT = [ctx.enter_context(nc.psum_tensor(f"YT{i}", [128, 3, 128], f32)) for i in range(CHUNKS)]

        ld_small, ld_tok, ld_patch, ld_const = sem("ld_small"), sem("ld_tok"), sem("ld_patch"), sem("ld_const")
        ld_mix, ld_out, ld_ffn = sem("ld_mix"), sem("ld_out"), sem("ld_ffn")
        full = [sem(f"full{i}") for i in range(BANKS)]
        names = """posf_made pads_made a_log_exp a_made wf_full wf_made
        h0_made xc1_made rln1 rs1_made xin_made xfb_made xpad_made conv_made u_made sz_made bcf_made bc_split bc_made
        sp_abs sp_exp sp_log sp_one sp_err sp_parts dt_made du_made a_ready b_made h_made p_made
        yT_full yT_copied y_skip y_gated ys_made mo_made h1_made xc2_made rln2 rs2_made h2_made t2_made
        tmw_made logits_made gate_in gate_exp hid_raw mix_read res_made out_done dve_chain pool_chain""".split()
        s = {n: sem(n) for n in names}

        PE_SLOTS = [
            [("y0", -1), ("c1", 1), ("up5", -2), ("y1", -1), ("dn0", -2), "turn", ("v1", 1), ("y2", -1), ("bc4", 0),
             ("dn1", -2), ("mo", -1), ("bc5", 0)],
            ["turn", ("in0", 1), ("in1", 1), ("xc0", 1), ("dn2", -2), ("xc1", 1), ("xc2", 1), ("c2", -1),
             ("bc6", 0), ("v2", -1), ("z0", 1)],
            ["turn", ("c3", -1), ("z1", 1), ("z2", 1), ("bc7", 0), ("v3", -1), ("xp", 1)],
            ["turn", ("dt0", 1), ("dt1", 1), ("dt2", 1), ("gate", -1)],
            ["turn", ("bc0", 1), ("tok", 2), ("bc1", 1), ("bc2", 1), ("bc3", 1), ("up0", -1), ("up1", -1),
             ("up2", -1), ("up3", -1), ("up4", -1)],
            ["turn"]]
        ACT_SLOTS = [
            [("bc4", 0), "decay", ("mo", -1), ("bc5", 0), ("in0", 1), ("in1", 1)],
            ["decay", ("xc0", 1), ("xc1", 1), ("c2", -1), ("xc2", 1), ("bc6", 0), ("v2", -1)],
            ["decay", ("z0", 1), ("c3", -1), ("z1", 1), ("z2", 1), ("bc7", 0), ("u0", 1), ("u1", 1), ("u2", 1),
             ("v3", -1)],
            ["decay", ("xp", 1), ("dt0", 1), ("dt1", 1), ("dt2", 1), ("gate", -1), ("dtb", 1), ("bc0", 1),
             ("tok", 2), ("bc1", 1), ("bc2", 1), ("bc3", 1)],
            ["decay", ("up0", -1), ("up1", -1), ("up2", -1), ("y0", 0), ("up3", -1), ("up4", -1), ("c1", 2),
             ("y1", 0), ("up5", -1)],
            ["decay", ("y2", 0), ("v1", 2)]]
        DVE_SLOTS = [
            ["scan1", ("y0", -1), ("dt2", 0), "scan2", ("mix0", -2), ("y1", -1), ("du2", 0), ("y2", -1), "scan3",
             ("mo", -1), ("mix1", -2)],
            ["scan1", "scan2", "scan3"],
            ["scan1", ("mix2", -2), ("conv0", 1), ("conv1", 1), "scan2", ("v2", -1), ("conv2", 1), "scan3",
             ("wf", 1), ("split", 1), ("v3", -1)],
            ["scan1", "scan2", ("gate", -1), "scan3"],
            ["scan1", ("gate2", -1), ("sp", 1), "scan2", "scan3", ("dt0", 1), ("du0", 1)],
            ["scan1", ("dt1", 1), ("v1", 2), ("du1", 1), "scan2", "scan3"]]
        POOL_SLOTS = [
            [("v1", 1), ("du2", 0), ("v2", -1), ("v3", -1), ("split", 1), ("dt0", 1), ("du0", 1), ("dt1", 1),
             ("dt2", 1), ("du1", 1), ("mo", 0)]]

        TILES = {
            "tok": (1, lambda g, i: ("h0_made", g + 1)),
            "c1": (1, lambda g, i: ("xc1_made", g + 1)),
            "v1": (1, lambda g, i: ("rln1", g + 1)),
            **{f"in{d}": (1, lambda g, i, d=d: ("xfb_made", 4 * g + 2 * d + 2)) for d in range(2)},
            **{f"xc{c}": (1, lambda g, i, c=c: ("xpad_made", CHUNKS * g + c + 1)) for c in range(CHUNKS)},
            **{f"z{c}": (1, lambda g, i, c=c: ("sz_made", CHUNKS * g + c + 1)) for c in range(CHUNKS)},
            "xp": (1, lambda g, i: ("bcf_made", g + 1)),
            **{f"dt{c}": (1, lambda g, i, c=c: ("sp_abs", CHUNKS * g + c + 1)) for c in range(CHUNKS)},
            **{f"bc{p}": (BCP, lambda g, i, p=p: ("bc_made", BCR * g + BCP * p + i + 1)) for p in range(BCR // BCP)},
            **{f"y{c}": (1, lambda g, i, c=c: ("y_skip", CHUNKS * g + c + 1)) for c in range(CHUNKS)},
            "mo": (1, lambda g, i: ("mo_made", 2 * g + 2)),
            "c2": (1, lambda g, i: ("xc2_made", 2 * g + 1)),
            "v2": (1, lambda g, i: ("rln2", 2 * g + 1)),
            "c3": (1, lambda g, i: ("xc2_made", 2 * g + 2)),
            "v3": (1, lambda g, i: ("rln2", 2 * g + 2)),
            "gate": (1, lambda g, i: ("logits_made", g + 1)),
            **{f"up{j}": (1, lambda g, i, j=j: ("hid_raw", FT * g + 3 * j + 3)) for j in range(FT // 3)},
            **{f"dn{e}": (1, lambda g, i, e=e: ("mix_read", EXPERTS * g + e + 1)) for e in range(EXPERTS)}}
        OFFSETS = [x[1] for table in (PE_SLOTS, ACT_SLOTS, DVE_SLOTS, POOL_SLOTS) for slot in table for x in slot
                   if not isinstance(x, str)]
        PERIODS = range(-max(OFFSETS), GROUPS - min(OFFSETS))
        BANK, FILL, LAST = {}, {}, {}
        for period in PERIODS:
            for slot in PE_SLOTS:
                for st, off in [x for x in slot if x != "turn" and x[0] in TILES and 0 <= period + x[1] < GROUPS]:
                    for i in range(TILES[st][0]):
                        n = len(BANK)
                        key = st, period + off, i
                        BANK[key], FILL[key] = n % BANKS, n // BANKS + 1
                        if n >= BANKS:
                            LAST[key] = read_by[n % BANKS]
                        else:
                            read_by = [] if n == 0 else read_by
                            read_by.append(None)
                        read_by[n % BANKS] = TILES[st][1](period + off, i)

        def program(slots, stages, scan):
            for g in PERIODS:
                for k in range(len(slots)):
                    for item in slots[k]:
                        if item in scan:
                            n = UNITS * g + k + {"decay": 2, "turn": -1}.get(item, 0)
                            if 0 <= n < UNITS * GROUPS:
                                scan[item](n)
                        elif 0 <= g + item[1] < GROUPS:
                            stages[item[0]](g + item[1])

        def on_vector(st, g):
            return g == 0 if st in FRONT_STEPS else g == GROUPS - 1

        FRONT_STEPS = ("v1", "split", "dt0", "dt1", "dt2", "du0", "du1", "du2")

        def small_steps(eng, E, then):
            def normed(out_, xc, rs):
                for m in range(2):
                    last = E.tensor_tensor(out_[:, m], xc[:, m], rs[:, 1], ALU.mult)
                return last

            def f_tok(g):
                eng.wait_ge(s["rs1_made"], g + 1)
                if g >= 2:
                    eng.wait_ge(s["h1_made"], g - 1)
                normed(xin[:, g % 2], xc1, rs1).then_inc(s["xin_made"], 1)

            def f_split(g):
                eng.wait_ge(s["bcf_made"], g + 1)
                bcr = bcf[0:3 * BCR]
                then(E.tensor_tensor(bcr, bcr, bc3[:], ALU.subtract))
                then(E.tensor_copy(bc3[BCR:2 * BCR], bcr[BCR:2 * BCR]))
                then(E.tensor_copy(bcm[2 * BCR:3 * BCR], bcr[2 * BCR:3 * BCR]))
                E.tensor_tensor(bc3[2 * BCR:3 * BCR], bcr[2 * BCR:3 * BCR], bcm[2 * BCR:3 * BCR], ALU.subtract)\
                    .then_inc(s["bc_split"], 1)
                eng.wait_ge(s["bc_split"], g + 1)

            def f_dt(g, c):
                eng.wait_ge(s["sp_parts"], g + 1)
                eng.wait_ge(s["sp_err"], g + 1)
                then(E.tensor_tensor(dt[:, c], dt[:, c], spl[:, c], ALU.add))
                then(E.tensor_tensor(spw[:, c], spw[:, c], spi[:, c], ALU.mult))
                E.tensor_tensor(dt[:, c], dt[:, c], spw[:, c], ALU.subtract).then_inc(s["dt_made"], 1)
                eng.wait_ge(s["dt_made"], CHUNKS * g + c + 1)

            def f_du(g, c):
                eng.wait_ge(s["u_made"], CHUNKS * g + c + 1)
                eng.wait_ge(s["dt_made"], CHUNKS * g + c + 1)
                if g:
                    eng.wait_ge(s["b_made"], UNITS * (g - 1) + CHUNKS + c + 1)
                E.tensor_tensor(du[:, c], dt[:, c], u[:, g % 2, c], ALU.mult).then_inc(s["du_made"], 1)

            def b_mo(g):
                eng.wait_ge(s["mo_made"], 2 * (g + 1))
                E.tensor_tensor(h1[:], h1[:], xin[:, g % 2], ALU.add).then_inc(s["h1_made"], 1)

            def b_ln(g):
                eng.wait_ge(s["rs2_made"], 2 * g + 1)
                then(normed(xc2, xc2, rs2))
                for m in range(2):
                    last = E.tensor_scalar(xc2[:, m], xc2[:, m], s96[:, S_LNG + m:][:, 0:1], s96[:, S_LNB + m:][:, 0:1],
                                           ALU.mult, ALU.add)
                then(last)
                if g:
                    eng.wait_ge(s["res_made"], g)
                E.tensor_tensor(h2[:], xc2[:], h0[:, g % 3], ALU.add).then_inc(s["h2_made"], 1)

            def b_ln2(g):
                eng.wait_ge(s["rs2_made"], 2 * g + 2)
                if g:
                    eng.wait_ge(s["out_done"], 16 * g)
                normed(t2, xc2, rs2).then_inc(s["t2_made"], 1)
            return {
                "v1": f_tok, "split": f_split, "mo": b_mo, "v2": b_ln, "v3": b_ln2,
                **{f"dt{c}": (lambda g, c=c: f_dt(g, c)) for c in range(CHUNKS)},
                **{f"du{c}": (lambda g, c=c: f_du(g, c)) for c in range(CHUNKS)}}

        block = ctx.enter_context(nc.Block())

        @block.sync
        def _(sp):
            def load_patches(g):
                if g:
                    sp.wait_ge(s["h0_made"], g)
                sp.dma_start(patches[:], xp[g]).then_inc(ld_patch, 16)
            sp.dma_start(s96[:], small96).then_inc(ld_small, 16)
            sp.dma_start(cst[:, 0:K_CD], consts[:, 0:K_CD]).then_inc(ld_small, 16)
            sp.dma_start(tokw_s[:], tokw).then_inc(ld_tok, 16)
            load_patches(0)
            sp.dma_start(cst[:, K_CD:], consts[:, K_CD:]).then_inc(ld_const, 16)
            sp.dma_start(s128[:], small128).then_inc(ld_const, 16)
            sp.dma_start(win_s[:], w_in).then_inc(ld_mix, 16)
            sp.dma_start(wmin_s[:], w_min).then_inc(ld_mix, 16)
            sp.dma_start(wxp_s[:], w_xp).then_inc(ld_mix, 16)
            sp.dma_start(wdt_s[3 * BCR:XPO, :], w_dt).then_inc(ld_mix, 16)
            sp.dma_start(sel_s[:], sel).then_inc(ld_mix, 16)
            sp.dma_start(wout_s, w_out).then_inc(ld_out, 16)
            sp.dma_start(wbmo_s, w_bmo).then_inc(ld_out, 16)
            sp.dma_start(w1_s[:], w1).then_inc(ld_ffn, 16)
            sp.dma_start(w2_s[:], w2).then_inc(ld_ffn, 16)
            for g in range(1, GROUPS):
                load_patches(g)
            for g in range(GROUPS):
                sp.wait_ge(s["res_made"], g + 1)
                sp.dma_start(out[g], res[:]).then_inc(s["out_done"], 16)
            sp.wait_ge(s["out_done"], 16 * GROUPS)
        LD_SMALL, LD_CONST, LD_MIX = 32, 32, 80

        @block.tensor
        def _(pe):
            mm = nc.tensor.matmul

            def tile(st, g, i=0):
                if (st, g, i) in LAST:
                    name, value = LAST[st, g, i]
                    pe.wait_ge(s[name], value)
                return PS[BANK[st, g, i]]

            def filled(ins, st, g, i=0):
                ins.then_inc(full[BANK[st, g, i]], 1)

            def centre(P, src):
                for m in range(2):
                    for k in range(2):
                        w = cst[0:HALF, (K_CD if k == m else K_CO):][:, 0:HALF]
                        last = mm(P[0:HALF, m * TOK:(m + 1) * TOK], lhsT=w, rhs=src[:, k], start=(k == 0), stop=(k == 1))
                return last

            def variance(P, sq):
                for k in range(2):
                    last = mm(P[0:HALF, 0:TOK], lhsT=cst[0:HALF, K_J:K_J + HALF], rhs=sq[:, k], start=(k == 0), stop=(k == 1))
                return last

            def f_tok(g):
                P = tile("tok", g)
                if g == 0:
                    pe.wait_ge(ld_small, LD_SMALL)
                    pe.wait_ge(ld_tok, 16)
                    pe.wait_ge(s["posf_made"], 1)
                pe.wait_ge(ld_patch, 16 * (g + 1))
                for m in range(2):
                    T = P[0:HALF, m * TOK:(m + 1) * TOK].rearrange("p (b l) -> p b l", b=GROUP)
                    mm(T, lhsT=cst[0:HALF, 0:HALF], rhs=posf[:, m:m + 1, :].broadcast_to([HALF, GROUP, LEN]), start=True, stop=False)
                    for k in range(PK):
                        last = mm(T[:, :, 2:LEN], lhsT=tokw_s[:, k, m * HALF:(m + 1) * HALF],
                                  rhs=patches[:, k].rearrange("p (b l) -> p b l", b=GROUP), start=False, stop=(k == PK - 1))
                filled(last, "tok", g)

            def f_centre(g):
                if g == 0:
                    pe.wait_ge(ld_const, LD_CONST)
                pe.wait_ge(s["h0_made"], g + 1)
                filled(centre(tile("c1", g), h0[:, g % 3]), "c1", g)

            def f_variance(g):
                pe.wait_ge(s["xc1_made"], g + 1)
                filled(variance(tile("v1", g), sq1), "v1", g)

            def f_in(g, d):
                if g == 0:
                    pe.wait_ge(ld_mix, LD_MIX)
                pe.wait_ge(s["xin_made"], g + 1)
                P = tile(f"in{d}", g)
                for m in range(2):
                    for k in range(2):
                        last = mm(P[0:HALF, m * TOK:(m + 1) * TOK], lhsT=win_s[:, k, d * DIM + m * HALF:][:, 0:HALF],
                                  rhs=xin[:, g % 2, k], start=(k == 0), stop=(k == 1))
                filled(last, f"in{d}", g)

            def proj_in(g, st, row):
                pe.wait_ge(s["xfb_made"], 4 * (g + 1))
                P = tile(st, g)
                for k in range(2):
                    last = mm(P[:, 0:STOK], lhsT=wmin_s[:, k, row * 128:(row + 1) * 128],
                              rhs=xfb[:, k].rearrange("p d b l -> p (d b l)"), start=(k == 0), stop=(k == 1))
                filled(last, st, g)

            def f_z(g, c):
                proj_in(g, f"z{c}", CHUNKS + c)
                if g == 0 and c == CHUNKS - 1:
                    fuse_out()

            def f_xp(g):
                pe.wait_ge(s["u_made"], CHUNKS * (g + 1))
                P = tile("xp", g)
                for c in range(CHUNKS):
                    last = mm(P[0:XPO, 0:STOK], lhsT=wxp_s[:, c], rhs=u[:, g % 2, c], start=(c == 0), stop=(c == CHUNKS - 1))
                filled(last, "xp", g)

            def f_dt(g, c):
                pe.wait_ge(s["bcf_made"], g + 1)
                P = tile(f"dt{c}", g)
                filled(mm(P[:, 0:STOK], lhsT=wdt_s[3 * BCR:XPO, c * 128:(c + 1) * 128], rhs=bcf[3 * BCR:XPO],
                          start=True, stop=True), f"dt{c}", g)

            def bc(g, p):
                pe.wait_ge(s["bc_split"], g + 1)
                for i in range(BCP):
                    half, j = (BCP * p + i) // (2 * NH), (BCP * p + i) % (2 * NH)
                    row = (j // NH) * STATE + half * NH + j % NH
                    P = tile(f"bc{p}", g, i)
                    filled(mm(P[:, 0:STOK], lhsT=sel_s[:, row:row + 1].broadcast_to([3 * BCR, 128]), rhs=bc3[:],
                              start=True, stop=True), f"bc{p}", g, i)

            def unit(ug):
                g, k = ug // UNITS, ug % UNITS
                half, c = k // CHUNKS, k % CHUNKS
                if ug == 0:
                    pe.wait_ge(s["wf_made"], 1)
                if half == 0 and g:
                    pe.wait_ge(s["yT_copied"], CHUNKS * (g - 1) + c + 1)
                pe.wait_ge(s["p_made"], ug + 1)
                for b in (0, 2, 1):
                    t0, n = BLOCKS[b]
                    for j in range(NH):
                        last = nc.tensor.matmul(YT[c][0:n, b], lhsT=hb[:, ug % HB, j, t0:t0 + n], rhs=ident,
                                                start=(half == 0 and b == 0 and j == 0),
                                                stop=(half == 1 and b == 1 and j == NH - 1), is_transpose=True)
                last.then_inc(s["yT_full"], 1)

            def y_back(g, c):
                pe.wait_ge(s["yT_copied"], CHUNKS * g + c + 1)
                P = tile(f"y{c}", g)
                for b, (t0, n) in enumerate(BLOCKS):
                    last = nc.tensor.transpose(P[:, t0:t0 + n], yTs[0:n, b], cst[0:n, K_ID:K_ID + n])
                filled(last, f"y{c}", g)

            def fuse_out():
                pe.wait_ge(ld_out, 32)
                for c in range(CHUNKS):
                    for k in range(2):
                        last = mm(YT[c][:, :, :].rearrange("p a b -> p (a b)")[:, 0:DIM], lhsT=wout_s[:, k, c * 128:(c + 1) * 128],
                                  rhs=wbmo_s[:, k], start=(k == 0), stop=(k == 1))
                last.then_inc(s["wf_full"], 1)

            def b_mo(g):
                pe.wait_ge(s["ys_made"], CHUNKS * (g + 1))
                P = tile("mo", g)
                for m in range(2):
                    for c in range(CHUNKS):
                        last = mm(P[0:HALF, m * TOK:(m + 1) * TOK], lhsT=wf[:, c, m * HALF:(m + 1) * HALF], rhs=ys[:, c],
                                  start=(c == 0), stop=(c == CHUNKS - 1))
                filled(last, "mo", g)

            def b_c2(g):
                pe.wait_ge(s["h1_made"], g + 1)
                filled(centre(tile("c2", g), h1), "c2", g)

            def b_v2(g):
                pe.wait_ge(s["xc2_made"], 2 * g + 1)
                filled(variance(tile("v2", g), sq2), "v2", g)

            def b_c3(g):
                pe.wait_ge(s["h2_made"], g + 1)
                filled(centre(tile("c3", g), h2), "c3", g)

            def b_v3(g):
                pe.wait_ge(s["xc2_made"], 2 * g + 2)
                filled(variance(tile("v3", g), sq2), "v3", g)

            def b_gate(g):
                pe.wait_ge(s["tmw_made"], g + 1)
                P = tile("gate", g)
                for k in range(2):
                    last = mm(P[:, 0:GROUP * EXPERTS], lhsT=cst[0:HALF, K_ONE:K_ONE + 128],
                              rhs=tmw[:, k].rearrange("p b e -> p (b e)"), start=(k == 0), stop=(k == 1))
                filled(last, "gate", g)

            def b_up(g, i):
                if g == 0 and i == 0:
                    pe.wait_ge(ld_ffn, 32)
                if i == 0:
                    pe.wait_ge(s["t2_made"], g + 1)
                P = tile(f"up{i}", g)
                for j in range(3):
                    for k in range(2):
                        last = mm(P[:, j * TOK:(j + 1) * TOK], lhsT=w1_s[:, k, (3 * i + j) * 128:(3 * i + j + 1) * 128],
                                  rhs=t2[:, k], start=(k == 0), stop=(k == 1))
                filled(last, f"up{i}", g)

            def b_down(g, e):
                pe.wait_ge(s["hid_raw"], FT * g + FPE * (e + 1))
                P = tile(f"dn{e}", g)
                for m in range(2):
                    for f in range(FPE):
                        last = mm(P[0:HALF, m * TOK:(m + 1) * TOK], lhsT=w2_s[:, e * FPE + f, m * HALF:(m + 1) * HALF],
                                  rhs=hid[:, e * FPE + f], start=(f == 0), stop=(f == FPE - 1))
                filled(last, f"dn{e}", g)

            program(PE_SLOTS, {
                "tok": f_tok, "c1": f_centre, "v1": f_variance, "xp": f_xp, "mo": b_mo, "c2": b_c2, "v2": b_v2,
                "c3": b_c3, "v3": b_v3, "gate": b_gate,
                **{f"in{d}": (lambda g, d=d: f_in(g, d)) for d in range(2)},
                **{f"xc{c}": (lambda g, c=c: proj_in(g, f"xc{c}", c)) for c in range(CHUNKS)},
                **{f"z{c}": (lambda g, c=c: f_z(g, c)) for c in range(CHUNKS)},
                **{f"dt{c}": (lambda g, c=c: f_dt(g, c)) for c in range(CHUNKS)},
                **{f"bc{p}": (lambda g, p=p: bc(g, p)) for p in range(BCR // BCP)},
                **{f"y{c}": (lambda g, c=c: y_back(g, c)) for c in range(CHUNKS)},
                **{f"up{i}": (lambda g, i=i: b_up(g, i)) for i in range(FT // 3)},
                **{f"dn{e}": (lambda g, e=e: b_down(g, e)) for e in range(EXPERTS)}}, {"turn": unit})

        @block.scalar
        def _(act):
            A = nc.scalar.activation

            def tile(st, g, i=0):
                act.wait_ge(full[BANK[st, g, i]], FILL[st, g, i])
                return PS[BANK[st, g, i]]

            LOG_EXP = "natural_log_exp_and_others"
            table = [None]

            def use(name):
                if name == LOG_EXP and table[0] != LOG_EXP:
                    act.preload_act_table_set(LOG_EXP)
                table[0] = name

            use(LOG_EXP)
            act.wait_ge(ld_const, LD_CONST)
            act.wait_ge(s["posf_made"], 1)
            A(Aneg[:], s128[:, C_ALOG:C_ALOG + CHUNKS * STATE], ACT.Exp).then_inc(s["a_log_exp"], 1)

            def f_tok(g):
                P = tile("tok", g)
                if g >= 3:
                    act.wait_ge(s["h2_made"], g - 2)
                A(h0[:, g % 3].rearrange("p m t -> p (m t)"), P[0:HALF, 0:2 * TOK], ACT.Copy).then_inc(s["h0_made"], 1)

            def f_centre(g):
                P = tile("c1", g)
                if g:
                    act.wait_ge(s["xin_made"], g)
                A(xc1[:].rearrange("p m t -> p (m t)"), P[0:HALF, 0:2 * TOK], ACT.Copy)
                A(sq1[:].rearrange("p m t -> p (m t)"), P[0:HALF, 0:2 * TOK], ACT.Square).then_inc(s["xc1_made"], 1)

            def f_variance(g):
                P = tile("v1", g)
                use(LOG_EXP)
                A(rs1[:, 0], P[0:HALF, 0:TOK], ACT.Ln, bias=eps[0:HALF, :]).then_inc(s["rln1"], 1)
                act.wait_ge(s["rln1"], g + 1)
                A(rs1[:, 1], rs1[:, 0], ACT.Exp, scale=-0.5).then_inc(s["rs1_made"], 1)

            def f_in(g, d):
                P = tile(f"in{d}", g)
                for m in range(2):
                    src = P[0:HALF, m * TOK:(m + 1) * TOK].rearrange("p (b l) -> p b l", b=GROUP)
                    dst = xfb[:, m, d] if d == 0 else xfb[:, m, d, :, ::-1]
                    A(dst, src, ACT.Identity, bias=s96[:, S_INB + 2 * d + m:][:, 0:1]).then_inc(s["xfb_made"], 1)

            def f_xc(g, c):
                if g == 0:
                    act.wait_ge(s["pads_made"], 1)
                P = tile(f"xc{c}", g)
                if g:
                    act.wait_ge(s["conv_made"], CHUNKS * (g - 1) + c + 1)
                A(xpad[:, c, :, TAPS - 1:], P[:, 0:STOK].rearrange("p (q l) -> p q l", q=SEQS), ACT.Copy)\
                    .then_inc(s["xpad_made"], 1)

            def f_z(g, c):
                P = tile(f"z{c}", g)
                if g >= 2:
                    act.wait_ge(s["y_gated"], CHUNKS * (g - 2) + c + 1)
                use("silu")
                A(sz[:, g % 2, c], P[:, 0:STOK], ACT.Silu).then_inc(s["sz_made"], 1)

            def f_u(g, c):
                act.wait_ge(s["conv_made"], CHUNKS * g + c + 1)
                if g >= 2:
                    act.wait_ge(s["y_skip"], CHUNKS * (g - 2) + c + 1)
                use("silu")
                A(u[:, g % 2, c], conv[:, c], ACT.Silu, bias=s128[:, C_CB + c:C_CB + c + 1]).then_inc(s["u_made"], 1)

            def f_xp(g):
                P = tile("xp", g)
                if g:
                    last = f"bc{BCR // BCP - 1}", g - 1, BCP - 1
                    act.wait_ge(full[BANK[last]], FILL[last])
                A(bc3[:], P[0:3 * BCR, 0:STOK], ACT.Copy)
                A(bcf[:], P[0:XPO, 0:STOK], ACT.Copy).then_inc(s["bcf_made"], 1)

            def f_dt(g, c):
                if g:
                    act.wait_ge(s["a_ready"], UNITS * g)
                if g >= 3:
                    last = f"dn{EXPERTS - 1}", g - 3, 0
                    act.wait_ge(full[BANK[last]], FILL[last])
                if g == 0:
                    act.wait_ge(s["wf_full"], 1)
                P = tile(f"dt{c}", g)
                bias = s128[:, C_DTB + c:C_DTB + c + 1]
                A(spe[:, c], P[:, 0:STOK], ACT.Abs, bias=bias)
                A(dt[:, c], P[:, 0:STOK], ACT.Relu, bias=bias).then_inc(s["sp_abs"], 1)

            def f_parts(g):
                act.wait_ge(s["sp_abs"], CHUNKS * (g + 1))
                use(LOG_EXP)
                A(spe, spe, ACT.Exp, scale=-1.0).then_inc(s["sp_exp"], 1)
                act.wait_ge(s["sp_exp"], g + 1)
                A(spl, spe, ACT.Ln, bias=1.0).then_inc(s["sp_log"], 1)
                A(spw[:], spe, ACT.Identity, bias=1.0).then_inc(s["sp_one"], 1)
                act.wait_ge(s["sp_log"], g + 1)
                A(spi, spl, ACT.Exp, scale=-1.0).then_inc(s["sp_parts"], 1)

            def bc(g, p):
                half = BCP * p // (2 * NH)
                if g and BCP * p % NH == 0:
                    is_b = BCP * p % (2 * NH) == 0
                    act.wait_ge(s["b_made" if is_b else "p_made"], UNITS * (g - 1) + CHUNKS * (half + 1))
                for i in range(BCP):
                    P = tile(f"bc{p}", g, i)
                    A(BC[:, half, (BCP * p + i) % (2 * NH)], P[:, 0:STOK], ACT.Copy).then_inc(s["bc_made"], 1)

            def ahead(ug):
                g, k = ug // UNITS, ug % UNITS
                half, c = k // CHUNKS, k % CHUNKS
                if ug == 0:
                    act.wait_ge(s["a_made"], 1)
                if half == 0:
                    act.wait_ge(s["dt_made"], CHUNKS * g + c + 1)
                if ug >= AB:
                    act.wait_ge(s["h_made"], ug - AB + 1)
                use(LOG_EXP)
                for j in range(NH):
                    n = c * STATE + half * NH + j
                    last = A(a[:, ug % AB, j, :, 1:LEN], dt[:, c].rearrange("p (q l) -> p q l", q=SEQS)[:, :, 1:LEN],
                             ACT.Exp, scale=Aneg[:, n:n + 1])
                last.then_inc(s["a_ready"], 1)

            def y_copy(g, c):
                act.wait_ge(s["yT_full"], UNITS * g + CHUNKS + c + 1)
                if CHUNKS * g + c:
                    n = CHUNKS * g + c - 1
                    last = f"y{n % CHUNKS}", n // CHUNKS, 0
                    act.wait_ge(full[BANK[last]], FILL[last])
                A(yTs[0:BLOCKS[0][1], 0:2], YT[c][0:BLOCKS[0][1], 0:2], ACT.Copy)
                A(yTs[0:BLOCKS[2][1], 2], YT[c][0:BLOCKS[2][1], 2], ACT.Copy).then_inc(s["yT_copied"], 1)

            def b_mo(g):
                P = tile("mo", g)
                if g:
                    act.wait_ge(s["t2_made"], g)
                for m in range(2):
                    A(h1[:, m], P[0:HALF, m * TOK:(m + 1) * TOK], ACT.Identity, bias=s96[:, S_OUTB + m:][:, 0:1])\
                        .then_inc(s["mo_made"], 1)

            def b_centre(g, which):
                P = tile(f"c{2 + which}", g)
                n = 2 * g + which
                if n:
                    act.wait_ge(s["t2_made" if which == 0 else "h2_made"], g if which == 0 else g + 1)
                A(xc2[:].rearrange("p m t -> p (m t)"), P[0:HALF, 0:2 * TOK], ACT.Copy)
                A(sq2[:].rearrange("p m t -> p (m t)"), P[0:HALF, 0:2 * TOK], ACT.Square).then_inc(s["xc2_made"], 1)

            def b_variance(g, which):
                P = tile(f"v{2 + which}", g)
                use(LOG_EXP)
                A(rs2[:, 0], P[0:HALF, 0:TOK], ACT.Ln, bias=eps[0:HALF, :]).then_inc(s["rln2"], 1)
                act.wait_ge(s["rln2"], 2 * g + which + 1)
                A(rs2[:, 1], rs2[:, 0], ACT.Exp, scale=-0.5).then_inc(s["rs2_made"], 1)

            def b_gate(g):
                act.wait_ge(s["gate_in"], g + 1)
                use(LOG_EXP)
                A(ge_[:], gl[:], ACT.Exp).then_inc(s["gate_exp"], 1)

            def b_up(g, i):
                if i == 0:
                    act.wait_ge(s["dt_made"], CHUNKS * min(g + 3, GROUPS))
                if g and i == 0:
                    last = f"dn{EXPERTS - 1}", g - 1, 0
                    act.wait_ge(full[BANK[last]], FILL[last])
                P = tile(f"up{i}", g)
                use("gelu")
                for j in range(3):
                    f = 3 * i + j
                    A(hid[:, f], P[:, j * TOK:(j + 1) * TOK], ACT.Gelu, bias=s128[:, C_B1 + f:C_B1 + f + 1])\
                        .then_inc(s["hid_raw"], 1)

            program(ACT_SLOTS, {
                "tok": f_tok, "c1": f_centre, "v1": f_variance, "xp": f_xp, "dtb": f_parts, "mo": b_mo,
                "c2": lambda g: b_centre(g, 0), "v2": lambda g: b_variance(g, 0),
                "c3": lambda g: b_centre(g, 1), "v3": lambda g: b_variance(g, 1), "gate": b_gate,
                **{f"in{d}": (lambda g, d=d: f_in(g, d)) for d in range(2)},
                **{f"xc{c}": (lambda g, c=c: f_xc(g, c)) for c in range(CHUNKS)},
                **{f"z{c}": (lambda g, c=c: f_z(g, c)) for c in range(CHUNKS)},
                **{f"u{c}": (lambda g, c=c: f_u(g, c)) for c in range(CHUNKS)},
                **{f"dt{c}": (lambda g, c=c: f_dt(g, c)) for c in range(CHUNKS)},
                **{f"bc{p}": (lambda g, p=p: bc(g, p)) for p in range(BCR // BCP)},
                **{f"y{c}": (lambda g, c=c: y_copy(g, c)) for c in range(CHUNKS)},
                **{f"up{i}": (lambda g, i=i: b_up(g, i)) for i in range(FT // 3)}}, {"decay": ahead})

        @block.vector
        def _(dve):
            V = nc.vector
            chain = [0]

            def then(ins):
                chain[0] += 1
                ins.then_inc(s["dve_chain"], 1)
                dve.wait_ge(s["dve_chain"], chain[0])

            def tile(st, g, i=0):
                dve.wait_ge(full[BANK[st, g, i]], FILL[st, g, i])
                return PS[BANK[st, g, i]]

            V.memset(eps[:], LN_EPS)
            dve.wait_ge(ld_small, LD_SMALL)
            V.tensor_copy(posf[:, :, 0:1], s96[:, S_CLS:S_CLS + 2].rearrange("p (m o) -> p m o", o=1))
            pos = s96[:, S_POS:S_POS + 74].rearrange("p (m l) -> p m l", m=2)
            V.tensor_tensor(posf[:, :, 1:2], pos[:, :, 0:1], s96[:, S_CT:S_CT + 2].rearrange("p (m o) -> p m o", o=1), ALU.add)
            V.tensor_tensor(posf[:, :, 2:LEN], pos[:, :, 1:37],
                            s96[:, S_TOKB:S_TOKB + 2].rearrange("p (m o) -> p m o", o=1).broadcast_to([HALF, 2, PATCHES]),
                            ALU.add).then_inc(s["posf_made"], 1)
            V.memset(xpad[:, :, :, 0:TAPS - 1], 0.0).then_inc(s["pads_made"], 1)
            dve.wait_ge(s["a_log_exp"], 1)
            V.tensor_scalar(Aneg[:], Aneg[:], -1.0, None, ALU.mult).then_inc(s["a_made"], 1)
            for i in range(AB):
                last = V.memset(a[:, i, :, :, 0:1], 0.0)
            then(last)

            def f_wf(g):
                if g == 0:
                    dve.wait_ge(s["wf_full"], 1)
                    for c in range(CHUNKS):
                        last = V.tensor_copy(wf[:, c], YT[c][:, :, :].rearrange("p a b -> p (a b)")[:, 0:DIM])
                    last.then_inc(s["wf_made"], 1)

            def scan1(ug):
                g, half, c = ug // UNITS, ug % UNITS // CHUNKS, ug % CHUNKS
                dve.wait_ge(s["bc_made"], BCR * g + 2 * NH * half + NH)
                if half == 0:
                    dve.wait_ge(s["du_made"], CHUNKS * g + c + 1)
                if ug >= HB:
                    dve.wait_ge(s["yT_full"], ug - HB + 1)
                V.tensor_tensor(hb[:, ug % HB], du[:, c:c + 1].broadcast_to([128, NH, STOK]), BC[:, half, 0:NH], ALU.mult)\
                    .then_inc(s["b_made"], 1)

            def scan2(ug):
                dve.wait_ge(s["b_made"], ug + 1)
                dve.wait_ge(s["a_ready"], ug + 1)
                flat = hb[:, ug % HB].rearrange("p n t -> p (n t)")
                V.tensor_tensor_scan(flat, a[:, ug % AB].rearrange("p n q l -> p (n q l)"), flat, 0.0, ALU.mult, ALU.add)\
                    .then_inc(s["h_made"], 1)

            def scan3(ug):
                g, half = ug // UNITS, ug % UNITS // CHUNKS
                dve.wait_ge(s["bc_made"], BCR * g + 2 * NH * (half + 1))
                dve.wait_ge(s["h_made"], ug + 1)
                V.tensor_tensor(hb[:, ug % HB], hb[:, ug % HB], BC[:, half, NH:2 * NH], ALU.mult).then_inc(s["p_made"], 1)

            def f_conv(g, c):
                dve.wait_ge(s["xpad_made"], CHUNKS * g + c + 1)
                if g:
                    dve.wait_ge(s["dt_made"], CHUNKS * (g - 1) + c + 1)
                C = conv[:, c].rearrange("p (q l) -> p q l", q=SEQS)
                tap = lambda k: (xpad[:, c, :, k:k + LEN], s128[:, C_CW + TAPS * c + k:][:, 0:1])
                then(V.tensor_scalar(C, *tap(0), None, ALU.mult))
                for k in range(1, TAPS):
                    ins = V.scalar_tensor_tensor(C, *tap(k), C, ALU.mult, ALU.add)
                    if k < TAPS - 1:
                        then(ins)
                ins.then_inc(s["conv_made"], 1)

            def f_dt(g):
                dve.wait_ge(s["sp_one"], g + 1)
                V.scalar_tensor_tensor(spw[:], spw[:], -1.0, spe, ALU.add, ALU.subtract).then_inc(s["sp_err"], 1)

            def y_finish(g, c):
                n = CHUNKS * g + c
                P = tile(f"y{c}", g)
                V.scalar_tensor_tensor(yg[:], u[:, g % 2, c], s128[:, C_D + c:C_D + c + 1], P[:, 0:STOK],
                                       ALU.mult, ALU.add).then_inc(s["y_skip"], 1)
                dve.wait_ge(s["y_skip"], n + 1)
                dve.wait_ge(s["sz_made"], n + 1)
                V.tensor_tensor(yg[:], yg[:], sz[:, g % 2, c], ALU.mult).then_inc(s["y_gated"], 1)
                dve.wait_ge(s["y_gated"], n + 1)
                if g:
                    dve.wait_ge(full[BANK["mo", g - 1, 0]], FILL["mo", g - 1, 0])
                y4 = yg[:].rearrange("p (d b l) -> p d b l", d=2, b=GROUP)
                V.tensor_tensor(ys[:, c].rearrange("p (b l) -> p b l", b=GROUP), y4[:, 0], y4[:, 1, :, ::-1], ALU.add)\
                    .then_inc(s["ys_made"], 1)
                dve.wait_ge(s["ys_made"], n + 1)

            def b_gate(g):
                dve.wait_ge(s["t2_made"], g + 1)
                then(V.reduce_sum(tm[:], t2[:].rearrange("p m (b l) -> p m b l", b=GROUP), AX.X))
                wgt = s96[:, S_WG:S_WG + 6].rearrange("p (m o e) -> p m o e", m=2, o=1)
                for m in range(2):
                    last = V.tensor_tensor(tmw[:, m], tm[:, m].rearrange("p (b o) -> p b o", o=1).broadcast_to([HALF, GROUP, EXPERTS]),
                                           wgt[:, m].broadcast_to([HALF, GROUP, EXPERTS]), ALU.mult)
                last.then_inc(s["tmw_made"], 1)

            def b_gate2(g):
                P = tile("gate", g)[:, 0:GROUP * EXPERTS].rearrange("p (b e) -> p b e", b=GROUP)
                V.tensor_scalar(gl[:], P, 1.0 / LEN, None, ALU.mult).then_inc(s["logits_made"], 1)
                dve.wait_ge(s["logits_made"], g + 1)
                bcast = lambda col: gm[:, :, col:col + 1].broadcast_to([128, GROUP, EXPERTS])
                then(V.reduce_max(gm[:, :, 0:1], gl[:], AX.X))
                V.tensor_tensor(gl[:], gl[:], bcast(0), ALU.subtract).then_inc(s["gate_in"], 1)
                dve.wait_ge(s["gate_exp"], g + 1)
                then(V.reduce_sum(gm[:, :, 1:2], ge_[:], AX.X))
                then(V.reciprocal(gm[:, :, 2:3], gm[:, :, 1:2]))
                then(V.tensor_tensor(ge_[:], ge_[:], bcast(2), ALU.mult))
                then(V.reduce_max(gm[:, :, 3:4], ge_[:], AX.X))
                then(V.tensor_tensor(gl[:], ge_[:], bcast(3), ALU.is_equal))
                then(V.tensor_scalar(gm[:, :, 0:1], gl[:, :, 0:1], -1.0, 1.0, ALU.mult, ALU.add))
                then(V.tensor_tensor(gl[:, :, 1:2], gl[:, :, 1:2], gm[:, :, 0:1], ALU.mult))
                then(V.tensor_tensor(gm[:, :, 1:2], gm[:, :, 0:1], gl[:, :, 1:2], ALU.subtract))
                then(V.tensor_tensor(gl[:, :, 2:3], gl[:, :, 2:3], gm[:, :, 1:2], ALU.mult))
                then(V.tensor_tensor(wg[:], ge_[:], gl[:], ALU.mult))

            def b_mix(g, e):
                P = tile(f"dn{e}", g)
                part = yg[0:HALF, :].rearrange("p (m b l) -> p m b l", m=2, b=GROUP)
                w = wg[0:HALF, :, e:e + 1].broadcast_to([HALF, GROUP, LEN])
                for m in range(2):
                    Y = P[0:HALF, m * TOK:(m + 1) * TOK].rearrange("p (b l) -> p b l", b=GROUP)
                    last = V.scalar_tensor_tensor(part[:, m], Y, s96[:, S_B2 + EXPERTS * m + e:][:, 0:1], w, ALU.add, ALU.mult)
                last.then_inc(s["mix_read"], 1)
                dve.wait_ge(s["mix_read"], EXPERTS * g + e + 1)
                flat = lambda t: t[:].rearrange("p m t -> p (m t)")
                if e < EXPERTS - 1:
                    then(V.tensor_tensor(flat(h2), flat(h2), yg[0:HALF, :], ALU.add))
                else:
                    V.tensor_tensor(flat(res), flat(h2), yg[0:HALF, :], ALU.add).then_inc(s["res_made"], 1)
                    dve.wait_ge(s["res_made"], g + 1)

            steps = small_steps(dve, V, then)
            program(DVE_SLOTS, {
                **{st: (lambda g, st=st: steps[st](g) if on_vector(st, g) else None) for st in steps},
                **{f"conv{c}": (lambda g, c=c: f_conv(g, c)) for c in range(CHUNKS)}, "sp": f_dt, "y0": lambda g: y_finish(g, 0), "y1": lambda g: y_finish(g, 1),
                "y2": lambda g: y_finish(g, 2), "gate": b_gate, "gate2": b_gate2,
                "wf": f_wf, **{f"mix{e}": (lambda g, e=e: b_mix(g, e)) for e in range(EXPERTS)}},
                {"scan1": scan1, "scan2": scan2, "scan3": scan3})

        @block.gpsimd
        def _(pool):
            G = nc.gpsimd
            chain = [0]

            def then(ins):
                chain[0] += 1
                ins.then_inc(s["pool_chain"], 1)
                pool.wait_ge(s["pool_chain"], chain[0])

            steps = small_steps(pool, G, then)
            program(POOL_SLOTS, {st: (lambda g, st=st: None if on_vector(st, g) else steps[st](g)) for st in steps}, {})


def kernel(**inputs):
    import ml_dtypes
    import numpy as np
    import concourse.bacc as bacc
    from concourse import mybir as _mybir
    from concourse.bass_utils import run_bass_kernel_spmd as run

    I = {k: np.asarray(v) for k, v in inputs.items()}
    f = lambda k: I[k]
    cc = np.ascontiguousarray

    def rows(w, p):
        return cc(w.reshape(w.shape[0] // p, p, -1).transpose(1, 0, 2))

    side = 96 // 16
    x = f("x").reshape(GROUPS, GROUP, 3, side, 16, side, 16).transpose(0, 2, 4, 6, 1, 3, 5)
    x = x.reshape(GROUPS, PK, 128, GROUP * PATCHES).transpose(0, 2, 1, 3)
    col = lambda v: rows(v.reshape(-1, 1), HALF)[:, :, 0]
    small96 = np.concatenate([
        rows(f("L0_tok_pos_embedding")[0].T, HALF).reshape(HALF, -1), col(f("L0_tok_b")), col(f("cls_tok")),
        col(f("L0_tok_class_token")), col(f("L0_attn_bm_in_b")), col(f("L0_attn_bm_out_b")), col(f("L0_attn_ln_g")),
        col(f("L0_attn_ln_b")), rows(f("L0_ffn_Wg").T, HALF).reshape(HALF, -1),
        rows(f("L0_ffn_b2").T, HALF).reshape(HALF, -1)], axis=1)
    ch = lambda v: rows(v.reshape(v.shape[0], -1), 128).reshape(128, -1)
    small128 = np.concatenate([
        ch(f("L0_attn_m_conv_w")), ch(f("L0_attn_m_conv_b")), ch(f("L0_attn_m_dt_b")), ch(f("L0_attn_m_A_log")),
        ch(f("L0_attn_m_D")), ch(f("L0_ffn_b1").reshape(-1))], axis=1)
    eye = np.eye(128, dtype=np.float32)
    consts = np.zeros((128, K_END), np.float32)
    consts[:, K_ID:K_ID + 128] = eye
    consts[:HALF, K_CD:K_CD + HALF] = eye[:HALF, :HALF] - np.float32(1.0 / DIM)
    consts[:HALF, K_CO:K_CO + HALF] = -np.float32(1.0 / DIM)
    consts[:HALF, K_J:K_J + HALF] = np.float32(1.0 / DIM)
    consts[:, K_ONE:K_ONE + 128] = 1.0
    sel = np.zeros((3 * BCR, BCR), ml_dtypes.bfloat16)
    for r in range(3 * BCR):
        sel[r, r % BCR] = 1
    xw = f("L0_attn_m_xproj_w").T
    xw = np.concatenate([xw[:, DT_RANK:]] * 3 + [xw[:, :DT_RANK]], axis=1)
    arrays = {
        "xp": x, "tokw": rows(f("L0_tok_W").T, 128), "small96": small96, "small128": small128, "consts": consts,
        "sel": sel, "w_in": rows(f("L0_attn_bm_in_w").T, HALF), "w_min": rows(f("L0_attn_m_in_w").T, HALF),
        "w_xp": rows(xw, 128), "w_dt": f("L0_attn_m_dt_w").T, "w_out": rows(f("L0_attn_m_out_w"), HALF),
        "w_bmo": rows(f("L0_attn_bm_out_w").T, HALF),
        "w1": rows(f("L0_ffn_W1").transpose(1, 0, 2).reshape(DIM, -1), HALF),
        "w2": rows(f("L0_ffn_W2").reshape(-1, DIM), 128)}
    nc = bacc.Bacc("TRN2", target_bir_lowering=False, num_devices=1)
    arrays = {f"in_{k}": cc(v) for k, v in arrays.items()}
    args = [nc.dram_tensor(k, v.shape, _mybir.dt.from_np(v.dtype), kind="ExternalInput").ap() for k, v in arrays.items()]
    args.append(nc.dram_tensor("out_0", (GROUPS, HALF, 2, TOK), _mybir.dt.float32, kind="ExternalOutput").ap())
    tower(nc, *args)
    r = run(nc, [arrays], core_ids=[0])
    got = r.results[0]["out_0"].reshape(GROUPS, HALF, 2, GROUP, LEN)
    return cc(got.transpose(0, 3, 4, 2, 1).reshape(BATCH, LEN, DIM))
```

```python
import concourse.bass as bass
from concourse import mybir
from contextlib import ExitStack

BATCH, LEN, DIM = 16, 38, 192
HALF = DIM // 2
PATCHES, PATCH_DIM = 36, 768
INNER, STATE, TAPS, DT_RANK = 384, 16, 4, 12
CHUNKS = INNER // 128
EXPERTS, HIDDEN = 3, 768
GROUP = 4
GROUPS = BATCH // GROUP
TOK = GROUP * LEN
SEQS = 2 * GROUP
STOK = SEQS * LEN
PK = PATCH_DIM // 128
NH = STATE // 2
UNITS = 2 * CHUNKS
FT = EXPERTS * HIDDEN // 128
FPE = HIDDEN // 128
BCR = 2 * STATE
BCP = 4
XPO = 3 * BCR + DT_RANK
BLOCKS = [(0, 3 * LEN), (3 * LEN, 3 * LEN), (6 * LEN, 2 * LEN)]
LN_EPS = 1e-5

S_POS, S_TOKB, S_CLS, S_CT, S_INB, S_OUTB, S_LNG, S_LNB, S_WG, S_B2, S_END = 0, 74, 76, 78, 80, 84, 86, 88, 90, 96, 102
C_CW, C_CB, C_DTB, C_ALOG, C_D, C_B1, C_END = 0, 12, 15, 18, 66, 69, 87
K_ID, K_CD, K_CO, K_J, K_ONE, K_END = 0, 128, 224, 320, 416, 544


def tower(nc, xp, tokw, small96, small128, consts, sel, w_in, w_min, w_xp, w_dt, w_out, w_bmo, w1, w2, out):
    f32, bf16 = mybir.dt.float32, mybir.dt.bfloat16
    ALU, ACT, AX = mybir.AluOpType, mybir.ActivationFunctionType, mybir.AxisListType
    with ExitStack() as ctx:
        def sb(name, shape, dt=f32):
            return ctx.enter_context(nc.sbuf_tensor(name, shape, dt))

        def sem(name):
            return ctx.enter_context(nc.semaphore(name))

        tokw_s = sb("tokw_s", [128, PK, DIM])
        s96 = sb("s96", [HALF, S_END])
        s128 = sb("s128", [128, C_END])
        cst = sb("cst", [128, K_END])
        sel_s = sb("sel_s", [3 * BCR, BCR], bf16)
        win_s = sb("win_s", [HALF, 2, 2 * DIM])
        wmin_s = sb("wmin_s", [HALF, 2, 2 * INNER])
        wxp_s = sb("wxp_s", [128, CHUNKS, XPO])
        wdt_s = sb("wdt_s", [128, INNER])
        w1_s = sb("w1_s", [HALF, 2, EXPERTS * HIDDEN])
        w2_s = sb("w2_s", [128, FT, DIM])
        ident = cst[:, K_ID:K_ID + 128]
        posf = sb("posf", [HALF, 2, LEN])
        eps = sb("eps", [128, 1])
        Aneg = sb("Aneg", [128, CHUNKS * STATE])
        wf = sb("wf", [128, CHUNKS, DIM])
        patches = sb("patches", [128, PK, GROUP * PATCHES])
        h0 = sb("h0", [HALF, 3, 2, TOK])
        xc1 = sb("xc1", [HALF, 2, TOK])
        sq1 = sb("sq1", [HALF, 2, TOK])
        rs1 = sq1
        xin = sb("xin", [HALF, 2, 2, TOK])
        xfb = sb("xfb", [HALF, 2, 2, GROUP, LEN])
        xpad = sb("xpad", [128, CHUNKS, SEQS, LEN + TAPS - 1])
        conv = sb("conv", [128, CHUNKS, STOK])
        spw = conv
        u = sb("u", [128, 2, CHUNKS, STOK])
        sz = sb("sz", [128, 2, CHUNKS, STOK])
        dt = sb("dt", [128, CHUNKS, STOK])
        du = sb("du", [128, CHUNKS, STOK])
        shared = sb("shared", [128, FT * TOK])
        hid = shared[:].rearrange("p (f t) -> p f t", f=FT)
        sp3 = shared[:].rearrange("p (k c t) -> p k c t", k=3, c=CHUNKS)
        spe, spl, spi = sp3[:, 0], sp3[:, 1], sp3[:, 2]
        wout_s = shared[0:HALF, 0:2 * INNER].rearrange("p (k n) -> p k n", k=2)
        wbmo_s = shared[0:HALF, 2 * INNER:2 * INNER + 2 * DIM].rearrange("p (k n) -> p k n", k=2)
        bcf = sb("bcf", [XPO, STOK])
        bc3 = sb("bc3", [3 * BCR, STOK], bf16)
        bcm = sb("bcm", [3 * BCR, STOK], bf16)
        BC = sb("BC", [128, 2, 2 * NH, STOK])
        AB, HB = 3, 2
        a = sb("a", [128, AB, NH, SEQS, LEN])
        hb = sb("hb", [128, HB, NH, STOK])
        yTs = sb("yTs", [128, 3, 128])
        yg = sb("yg", [128, STOK])
        ys = sb("ys", [128, CHUNKS, TOK])
        h1 = sb("h1", [HALF, 2, TOK])
        xc2 = h1
        sq2 = sb("sq2", [HALF, 2, TOK])
        rs2 = sq2
        h2 = sb("h2", [HALF, 2, TOK])
        t2 = sb("t2", [HALF, 2, TOK])
        tm = sb("tm", [HALF, 2, GROUP])
        tmw = sb("tmw", [HALF, 2, GROUP, EXPERTS])
        gl = sb("gl", [128, GROUP, EXPERTS])
        gm = sb("gm", [128, GROUP, 4])
        ge_ = sb("ge_", [128, GROUP, EXPERTS])
        wg = sb("wg", [128, GROUP, EXPERTS])
        res = t2

        BANKS = 5
        PS = [ctx.enter_context(nc.psum_tensor(f"PS{i}", [128, 512], f32)) for i in range(BANKS)]
        YT = [ctx.enter_context(nc.psum_tensor(f"YT{i}", [128, 3, 128], f32)) for i in range(CHUNKS)]

        ld_small, ld_tok, ld_patch, ld_const = sem("ld_small"), sem("ld_tok"), sem("ld_patch"), sem("ld_const")
        ld_mix, ld_out, ld_ffn = sem("ld_mix"), sem("ld_out"), sem("ld_ffn")
        full = [sem(f"full{i}") for i in range(BANKS)]
        names = """posf_made pads_made a_log_exp a_made wf_full wf_made
        h0_made xc1_made rln1 rs1_made xin_made xfb_made xpad_made conv_made u_made sz_made bcf_made bc_split bc_made
        sp_abs sp_exp sp_log sp_one sp_err sp_parts dt_made du_made a_ready b_made h_made p_made
        yT_full yT_copied y_skip y_gated ys_made mo_made h1_made xc2_made rln2 rs2_made h2_made t2_made
        w_made gate_top tmw_made logits_made gate_in gate_exp hid_raw mix_read
        res_made out_done dve_chain pool_chain""".split()
        s = {n: sem(n) for n in names}

        PE_SLOTS = [
            [("v1", 1), "turn", ("y2", -1), ("bc4", 0), ("bc5", 0), ("dn1", -2), ("mo", -1)],
            ["turn", ("in0", 1), ("in1", 1), ("dn2", -2), ("xc0", 1), ("c2", -1), ("xc1", 1), ("xc2", 1),
             ("v2", -1), ("z0", 1), ("z1", 1)],
            ["turn", ("c3", -1), ("bc6", 0), ("v3", -1), ("z2", 1), ("xp", 1), ("bc7", 0), ("dt0", 1), ("dt1", 1),
             ("dt2", 1), ("gate", -1)],
            ["turn", ("tok", 2), ("bc0", 1)],
            ["turn", ("bc1", 1), ("bc2", 1), ("bc3", 1), ("up0", -1), ("up1", -1), ("up2", -1), ("up3", -1),
             ("up4", -1), ("c1", 2)],
            ["turn", ("y0", 0), ("up5", -1), ("y1", 0), ("dn0", -1)]]
        ACT_SLOTS = [
            [("y2", -1), ("bc4", 0), ("bc5", 0), ("mo", -1), "decay", ("in0", 1), ("in1", 1)],
            ["decay", ("c2", -1), ("xc0", 1), ("xc1", 1), ("xc2", 1), ("v2", -1)],
            ["decay", ("u0", 1), ("c3", -1), ("z0", 1), ("z1", 1), ("bc6", 0), ("u1", 1), ("u2", 1), ("z2", 1),
             ("v3", -1), ("xp", 1), ("bc7", 0)],
            ["decay", ("logits", -1), ("dt0", 1), ("dt1", 1), ("dtb0", 1), ("dt2", 1), ("dtb1", 1), ("gate", -1),
             ("dtb2", 1), ("tok", 2), ("bc0", 1), ("bc1", 1), ("bc2", 1), ("y0", 0), ("bc3", 1)],
            ["decay", ("up0", -1), ("up1", -1), ("c1", 2), ("up2", -1), ("up3", -1), ("y1", 0), ("up4", -1),
             ("up5", -1)],
            ["decay", ("v1", 2)]]
        DVE_SLOTS = [
            [("wf", 0), "scan1", ("y0", -1), "scan2", ("y1", -1), ("mix0", -2), ("y2", -1), "scan3"],
            ["scan1", "scan2", ("du2", 0), ("mix1", -2), "scan3", ("mo", -1)],
            ["scan1", ("mix2", -2), ("conv0", 1), ("v1", 2), ("v2", -1), "scan2", ("conv1", 1), ("conv2", 1),
             ("sp0", 1), ("v3", -1), "scan3", ("dt0", 1)],
            ["scan1", ("gate", -1), ("split", 1), ("sp1", 1), "scan2", "scan3", ("gate2", -1)],
            ["scan1", ("dt1", 1), ("du0", 1), ("sp2", 1), "scan2", ("gate3", -1), ("du1", 1), "scan3"],
            ["scan1", ("dt2", 1), "scan2", "scan3"]]
        POOL_SLOTS = [
            [("v2", -1), ("v3", -1), ("split", 1), ("dt0", 1), ("dt1", 1), ("dt2", 1), ("gate3", -1), ("du0", 1),
             ("du1", 1), ("du2", 1), ("mo", 0), ("v1", 2)]]

        TILES = {
            "tok": (1, lambda g, i: ("h0_made", g + 1)),
            "c1": (1, lambda g, i: ("xc1_made", g + 1)),
            "v1": (1, lambda g, i: ("rln1", g + 1)),
            **{f"in{d}": (1, lambda g, i, d=d: ("xfb_made", 4 * g + 2 * d + 2)) for d in range(2)},
            **{f"xc{c}": (1, lambda g, i, c=c: ("xpad_made", CHUNKS * g + c + 1)) for c in range(CHUNKS)},
            **{f"z{c}": (1, lambda g, i, c=c: ("sz_made", CHUNKS * g + c + 1)) for c in range(CHUNKS)},
            "xp": (1, lambda g, i: ("bcf_made", g + 1)),
            **{f"dt{c}": (1, lambda g, i, c=c: ("sp_abs", CHUNKS * g + c + 1)) for c in range(CHUNKS)},
            **{f"bc{p}": (BCP, lambda g, i, p=p: ("bc_made", BCR * g + BCP * p + i + 1)) for p in range(BCR // BCP)},
            **{f"y{c}": (1, lambda g, i, c=c: ("y_skip", CHUNKS * g + c + 1)) for c in range(CHUNKS)},
            "mo": (1, lambda g, i: ("mo_made", 2 * g + 2)),
            "c2": (1, lambda g, i: ("xc2_made", 2 * g + 1)),
            "v2": (1, lambda g, i: ("rln2", 2 * g + 1)),
            "c3": (1, lambda g, i: ("xc2_made", 2 * g + 2)),
            "v3": (1, lambda g, i: ("rln2", 2 * g + 2)),
            "gate": (1, lambda g, i: ("logits_made", g + 1)),
            **{f"up{j}": (1, lambda g, i, j=j: ("hid_raw", FT * g + 3 * j + 3)) for j in range(FT // 3)},
            **{f"dn{e}": (1, lambda g, i, e=e: ("mix_read", EXPERTS * g + e + 1)) for e in range(EXPERTS)}}
        OFFSETS = [x[1] for table in (PE_SLOTS, ACT_SLOTS, DVE_SLOTS, POOL_SLOTS) for slot in table for x in slot
                   if not isinstance(x, str)]
        PERIODS = range(-max(OFFSETS), GROUPS - min(OFFSETS))
        BANK, FILL, LAST, read_by = {}, {}, {}, [None] * BANKS
        for period in PERIODS:
            for slot in PE_SLOTS:
                for st, off in [x for x in slot if x != "turn" and x[0] in TILES and 0 <= period + x[1] < GROUPS]:
                    for i in range(TILES[st][0]):
                        n = len(BANK)
                        key = st, period + off, i
                        BANK[key], FILL[key] = n % BANKS, n // BANKS + 1
                        if n >= BANKS:
                            LAST[key] = read_by[n % BANKS]
                        read_by[n % BANKS] = TILES[st][1](period + off, i)

        def steps_of(slots):
            for g in PERIODS:
                for k in range(len(slots)):
                    for item in slots[k]:
                        if isinstance(item, str):
                            n = UNITS * g + k + {"decay": 2, "turn": -1}.get(item, 0)
                            if 0 <= n < UNITS * GROUPS:
                                yield item, n
                        elif 0 <= g + item[1] < GROUPS:
                            yield item[0], g + item[1]

        def parts_chunks(g, c):
            return slice(c, c + 1) if g == 0 else slice(0, CHUNKS) if c == CHUNKS - 1 else None

        def parts_count(g, c):
            return c + 1 if g == 0 else CHUNKS + g

        def on_vector(st, g):
            return g == 0 if st in FRONT_STEPS else g == GROUPS - 1

        FRONT_STEPS = ("v1", "split", "dt0", "dt1", "dt2", "du0", "du1", "du2")

        def small_steps(eng, E, then):
            def normed(out_, xc, rs):
                for m in range(2):
                    last = E.tensor_tensor(out_[:, m], xc[:, m], rs[:, 1], ALU.mult)
                return last

            def f_tok(g):
                eng.wait_ge(s["rs1_made"], g + 1)
                if g >= 2:
                    eng.wait_ge(s["h1_made"], g - 1)
                normed(xin[:, g % 2], xc1, rs1).then_inc(s["xin_made"], 1)

            def f_split(g):
                eng.wait_ge(s["bcf_made"], g + 1)
                bcr = bcf[0:3 * BCR]
                then(E.tensor_tensor(bcr, bcr, bc3[:], ALU.subtract))
                then(E.tensor_copy(bc3[BCR:2 * BCR], bcr[BCR:2 * BCR]))
                then(E.tensor_copy(bcm[2 * BCR:3 * BCR], bcr[2 * BCR:3 * BCR]))
                E.tensor_tensor(bc3[2 * BCR:3 * BCR], bcr[2 * BCR:3 * BCR], bcm[2 * BCR:3 * BCR], ALU.subtract)\
                    .then_inc(s["bc_split"], 1)
                eng.wait_ge(s["bc_split"], g + 1)

            def f_dt(g, c):
                eng.wait_ge(s["sp_parts"], parts_count(g, c))
                eng.wait_ge(s["sp_err"], parts_count(g, c))
                then(E.tensor_tensor(dt[:, c], dt[:, c], spl[:, c], ALU.add))
                then(E.tensor_tensor(spw[:, c], spw[:, c], spi[:, c], ALU.mult))
                E.tensor_tensor(dt[:, c], dt[:, c], spw[:, c], ALU.subtract).then_inc(s["dt_made"], 1)
                eng.wait_ge(s["dt_made"], CHUNKS * g + c + 1)

            def f_du(g, c):
                eng.wait_ge(s["u_made"], CHUNKS * g + c + 1)
                eng.wait_ge(s["dt_made"], CHUNKS * g + c + 1)
                if g:
                    eng.wait_ge(s["b_made"], UNITS * (g - 1) + CHUNKS + c + 1)
                E.tensor_tensor(du[:, c], dt[:, c], u[:, g % 2, c], ALU.mult).then_inc(s["du_made"], 1)

            def b_mo(g):
                eng.wait_ge(s["mo_made"], 2 * (g + 1))
                E.tensor_tensor(h1[:], h1[:], xin[:, g % 2], ALU.add).then_inc(s["h1_made"], 1)

            def b_ln(g):
                eng.wait_ge(s["rs2_made"], 2 * g + 1)
                then(normed(xc2, xc2, rs2))
                for m in range(2):
                    last = E.tensor_scalar(xc2[:, m], xc2[:, m], s96[:, S_LNG + m:][:, 0:1], s96[:, S_LNB + m:][:, 0:1],
                                           ALU.mult, ALU.add)
                then(last)
                if g:
                    eng.wait_ge(s["res_made"], g)
                E.tensor_tensor(h2[:], xc2[:], h0[:, g % 3], ALU.add).then_inc(s["h2_made"], 1)

            def b_gate3(g):
                eng.wait_ge(s["gate_top"], g + 1)
                then(E.tensor_scalar(gm[:, :, 0:1], gl[:, :, 0:1], -1.0, 1.0, ALU.mult, ALU.add))
                then(E.tensor_tensor(gl[:, :, 1:2], gl[:, :, 1:2], gm[:, :, 0:1], ALU.mult))
                then(E.tensor_tensor(gm[:, :, 1:2], gm[:, :, 0:1], gl[:, :, 1:2], ALU.subtract))
                then(E.tensor_tensor(gl[:, :, 2:3], gl[:, :, 2:3], gm[:, :, 1:2], ALU.mult))
                if g:
                    eng.wait_ge(s["mix_read"], EXPERTS * g)
                E.tensor_tensor(wg[:], ge_[:], gl[:], ALU.mult).then_inc(s["w_made"], 1)

            def b_ln2(g):
                eng.wait_ge(s["rs2_made"], 2 * g + 2)
                if g:
                    eng.wait_ge(s["out_done"], 16 * g)
                normed(t2, xc2, rs2).then_inc(s["t2_made"], 1)

            return {
                "v1": f_tok, "split": f_split, "mo": b_mo, "v2": b_ln, "v3": b_ln2, "gate3": b_gate3,
                **{f"dt{c}": (lambda g, c=c: f_dt(g, c)) for c in range(CHUNKS)},
                **{f"du{c}": (lambda g, c=c: f_du(g, c)) for c in range(CHUNKS)}}

        block = ctx.enter_context(nc.Block())

        @block.sync
        def _(sp):
            def load_patches(g):
                if g:
                    sp.wait_ge(s["h0_made"], g)
                sp.dma_start(patches[:], xp[g]).then_inc(ld_patch, 16)
            sp.dma_start(s96[:], small96).then_inc(ld_small, 16)
            sp.dma_start(cst[:, 0:K_CD], consts[:, 0:K_CD]).then_inc(ld_small, 16)
            sp.dma_start(tokw_s[:], tokw).then_inc(ld_tok, 16)
            load_patches(0)
            sp.dma_start(cst[:, K_CD:], consts[:, K_CD:]).then_inc(ld_const, 16)
            sp.dma_start(s128[:], small128).then_inc(ld_const, 16)
            sp.dma_start(win_s[:], w_in).then_inc(ld_mix, 16)
            sp.dma_start(wmin_s[:], w_min).then_inc(ld_mix, 16)
            sp.dma_start(wxp_s[:], w_xp).then_inc(ld_mix, 16)
            sp.dma_start(wdt_s[3 * BCR:XPO, :], w_dt).then_inc(ld_mix, 16)
            sp.dma_start(sel_s[:], sel).then_inc(ld_mix, 16)
            sp.dma_start(wout_s, w_out).then_inc(ld_out, 16)
            sp.dma_start(wbmo_s, w_bmo).then_inc(ld_out, 16)
            sp.dma_start(w1_s[:], w1).then_inc(ld_ffn, 16)
            sp.dma_start(w2_s[:], w2).then_inc(ld_ffn, 16)
            for g in range(1, GROUPS):
                load_patches(g)
            for g in range(GROUPS):
                sp.wait_ge(s["res_made"], g + 1)
                sp.dma_start(out[g], res[:]).then_inc(s["out_done"], 16)
            sp.wait_ge(s["out_done"], 16 * GROUPS)
        LD_SMALL, LD_CONST, LD_MIX = 32, 32, 80

        @block.tensor
        def _(pe):
            mm = nc.tensor.matmul

            def tile(st, g, i=0):
                if (st, g, i) in LAST:
                    name, value = LAST[st, g, i]
                    pe.wait_ge(s[name], value)
                return PS[BANK[st, g, i]]

            def filled(ins, st, g, i=0):
                ins.then_inc(full[BANK[st, g, i]], 1)

            def centre(P, src):
                for m in range(2):
                    for k in range(2):
                        w = cst[0:HALF, (K_CD if k == m else K_CO):][:, 0:HALF]
                        last = mm(P[0:HALF, m * TOK:(m + 1) * TOK], lhsT=w, rhs=src[:, k], start=(k == 0), stop=(k == 1))
                return last

            def variance(P, sq):
                for k in range(2):
                    last = mm(P[0:HALF, 0:TOK], lhsT=cst[0:HALF, K_J:K_J + HALF], rhs=sq[:, k], start=(k == 0), stop=(k == 1))
                return last

            def f_tok(g):
                P = tile("tok", g)
                if g == 0:
                    pe.wait_ge(ld_small, LD_SMALL)
                    pe.wait_ge(ld_tok, 16)
                    pe.wait_ge(s["posf_made"], 1)
                pe.wait_ge(ld_patch, 16 * (g + 1))
                for m in range(2):
                    T = P[0:HALF, m * TOK:(m + 1) * TOK].rearrange("p (b l) -> p b l", b=GROUP)
                    mm(T, lhsT=cst[0:HALF, 0:HALF], rhs=posf[:, m:m + 1, :].broadcast_to([HALF, GROUP, LEN]),
                       start=True, stop=False)
                    for k in range(PK):
                        last = mm(T[:, :, 2:LEN], lhsT=tokw_s[:, k, m * HALF:(m + 1) * HALF],
                                  rhs=patches[:, k].rearrange("p (b l) -> p b l", b=GROUP), start=False, stop=(k == PK - 1))
                filled(last, "tok", g)

            def f_centre(g):
                if g == 0:
                    pe.wait_ge(ld_const, LD_CONST)
                pe.wait_ge(s["h0_made"], g + 1)
                filled(centre(tile("c1", g), h0[:, g % 3]), "c1", g)

            def f_variance(g):
                pe.wait_ge(s["xc1_made"], g + 1)
                filled(variance(tile("v1", g), sq1), "v1", g)

            def f_in(g, d):
                if g == 0:
                    pe.wait_ge(ld_mix, LD_MIX)
                pe.wait_ge(s["xin_made"], g + 1)
                P = tile(f"in{d}", g)
                for m in range(2):
                    for k in range(2):
                        last = mm(P[0:HALF, m * TOK:(m + 1) * TOK], lhsT=win_s[:, k, d * DIM + m * HALF:][:, 0:HALF],
                                  rhs=xin[:, g % 2, k], start=(k == 0), stop=(k == 1))
                filled(last, f"in{d}", g)

            def proj_in(g, st, row):
                pe.wait_ge(s["xfb_made"], 4 * (g + 1))
                P = tile(st, g)
                for k in range(2):
                    last = mm(P[:, 0:STOK], lhsT=wmin_s[:, k, row * 128:(row + 1) * 128],
                              rhs=xfb[:, k].rearrange("p d b l -> p (d b l)"), start=(k == 0), stop=(k == 1))
                filled(last, st, g)

            def f_z(g, c):
                proj_in(g, f"z{c}", CHUNKS + c)
                if g == 0 and c == CHUNKS - 1:
                    fuse_out()

            def f_xp(g):
                pe.wait_ge(s["u_made"], CHUNKS * (g + 1))
                P = tile("xp", g)
                for c in range(CHUNKS):
                    last = mm(P[0:XPO, 0:STOK], lhsT=wxp_s[:, c], rhs=u[:, g % 2, c], start=(c == 0), stop=(c == CHUNKS - 1))
                filled(last, "xp", g)

            def f_dt(g, c):
                pe.wait_ge(s["bcf_made"], g + 1)
                P = tile(f"dt{c}", g)
                filled(mm(P[:, 0:STOK], lhsT=wdt_s[3 * BCR:XPO, c * 128:(c + 1) * 128], rhs=bcf[3 * BCR:XPO],
                          start=True, stop=True), f"dt{c}", g)

            def bc(g, p):
                pe.wait_ge(s["bc_split"], g + 1)
                for i in range(BCP):
                    half, j = (BCP * p + i) // (2 * NH), (BCP * p + i) % (2 * NH)
                    row = (j // NH) * STATE + half * NH + j % NH
                    P = tile(f"bc{p}", g, i)
                    filled(mm(P[:, 0:STOK], lhsT=sel_s[:, row:row + 1].broadcast_to([3 * BCR, 128]), rhs=bc3[:],
                              start=True, stop=True), f"bc{p}", g, i)

            def unit(ug):
                g, k = ug // UNITS, ug % UNITS
                half, c = k // CHUNKS, k % CHUNKS
                if ug == 0:
                    pe.wait_ge(s["wf_made"], 1)
                if half == 0 and g:
                    pe.wait_ge(s["yT_copied"], CHUNKS * (g - 1) + c + 1)
                pe.wait_ge(s["p_made"], ug + 1)
                for b in (0, 2, 1):
                    t0, n = BLOCKS[b]
                    for j in range(NH):
                        last = nc.tensor.matmul(YT[c][0:n, b], lhsT=hb[:, ug % HB, j, t0:t0 + n], rhs=ident,
                                                start=(half == 0 and b == 0 and j == 0),
                                                stop=(half == 1 and b == 1 and j == NH - 1), is_transpose=True)
                last.then_inc(s["yT_full"], 1)

            def y_back(g, c):
                pe.wait_ge(s["yT_copied"], CHUNKS * g + c + 1)
                P = tile(f"y{c}", g)
                for b, (t0, n) in enumerate(BLOCKS):
                    last = nc.tensor.transpose(P[:, t0:t0 + n], yTs[0:n, b], cst[0:n, K_ID:K_ID + n])
                filled(last, f"y{c}", g)

            def fuse_out():
                pe.wait_ge(ld_out, 32)
                for c in range(CHUNKS):
                    for k in range(2):
                        last = mm(YT[c][:, :, :].rearrange("p a b -> p (a b)")[:, 0:DIM],
                                  lhsT=wout_s[:, k, c * 128:(c + 1) * 128], rhs=wbmo_s[:, k], start=(k == 0), stop=(k == 1))
                last.then_inc(s["wf_full"], 1)

            def b_mo(g):
                pe.wait_ge(s["ys_made"], CHUNKS * (g + 1))
                P = tile("mo", g)
                for m in range(2):
                    for c in range(CHUNKS):
                        last = mm(P[0:HALF, m * TOK:(m + 1) * TOK], lhsT=wf[:, c, m * HALF:(m + 1) * HALF], rhs=ys[:, c],
                                  start=(c == 0), stop=(c == CHUNKS - 1))
                filled(last, "mo", g)

            def b_c2(g):
                pe.wait_ge(s["h1_made"], g + 1)
                filled(centre(tile("c2", g), h1), "c2", g)

            def b_v2(g):
                pe.wait_ge(s["xc2_made"], 2 * g + 1)
                filled(variance(tile("v2", g), sq2), "v2", g)

            def b_c3(g):
                pe.wait_ge(s["h2_made"], g + 1)
                filled(centre(tile("c3", g), h2), "c3", g)

            def b_v3(g):
                pe.wait_ge(s["xc2_made"], 2 * g + 2)
                filled(variance(tile("v3", g), sq2), "v3", g)

            def b_gate(g):
                pe.wait_ge(s["tmw_made"], g + 1)
                P = tile("gate", g)
                for k in range(2):
                    last = mm(P[:, 0:GROUP * EXPERTS], lhsT=cst[0:HALF, K_ONE:K_ONE + 128],
                              rhs=tmw[:, k].rearrange("p b e -> p (b e)"), start=(k == 0), stop=(k == 1))
                filled(last, "gate", g)

            def b_up(g, i):
                if g == 0 and i == 0:
                    pe.wait_ge(ld_ffn, 32)
                if i == 0:
                    pe.wait_ge(s["t2_made"], g + 1)
                P = tile(f"up{i}", g)
                for j in range(3):
                    for k in range(2):
                        last = mm(P[:, j * TOK:(j + 1) * TOK], lhsT=w1_s[:, k, (3 * i + j) * 128:(3 * i + j + 1) * 128],
                                  rhs=t2[:, k], start=(k == 0), stop=(k == 1))
                filled(last, f"up{i}", g)

            def b_down(g, e):
                pe.wait_ge(s["hid_raw"], FT * g + FPE * (e + 1))
                P = tile(f"dn{e}", g)
                for m in range(2):
                    for f in range(FPE):
                        last = mm(P[0:HALF, m * TOK:(m + 1) * TOK], lhsT=w2_s[:, e * FPE + f, m * HALF:(m + 1) * HALF],
                                  rhs=hid[:, e * FPE + f], start=(f == 0), stop=(f == FPE - 1))
                filled(last, f"dn{e}", g)

            steps = {
                "tok": f_tok, "c1": f_centre, "v1": f_variance, "xp": f_xp, "mo": b_mo, "c2": b_c2, "v2": b_v2,
                "c3": b_c3, "v3": b_v3, "gate": b_gate,
                **{f"in{d}": (lambda g, d=d: f_in(g, d)) for d in range(2)},
                **{f"xc{c}": (lambda g, c=c: proj_in(g, f"xc{c}", c)) for c in range(CHUNKS)},
                **{f"z{c}": (lambda g, c=c: f_z(g, c)) for c in range(CHUNKS)},
                **{f"dt{c}": (lambda g, c=c: f_dt(g, c)) for c in range(CHUNKS)},
                **{f"bc{p}": (lambda g, p=p: bc(g, p)) for p in range(BCR // BCP)},
                **{f"y{c}": (lambda g, c=c: y_back(g, c)) for c in range(CHUNKS)},
                **{f"up{i}": (lambda g, i=i: b_up(g, i)) for i in range(FT // 3)},
                **{f"dn{e}": (lambda g, e=e: b_down(g, e)) for e in range(EXPERTS)}, "turn": unit}
            for st, g in steps_of(PE_SLOTS):
                steps[st](g)

        @block.scalar
        def _(act):
            A = nc.scalar.activation

            def tile(st, g, i=0):
                act.wait_ge(full[BANK[st, g, i]], FILL[st, g, i])
                return PS[BANK[st, g, i]]

            LOG_EXP = "natural_log_exp_and_others"
            SET_OF = {**{st: LOG_EXP for st in ("v1", "v2", "v3", "gate", "dtb0", "dtb1", "dtb2", "decay")},
                      **{f"{st}{c}": "silu_and_others" for st in "zu" for c in range(CHUNKS)},
                      **{f"up{i}": "gelu_and_others" for i in range(FT // 3)}}

            def tables_ahead(held, later):
                wanted = next((SET_OF[st] for st, _ in later if st in SET_OF), held)
                if wanted != held:
                    act.preload_act_table_set(wanted)
                return wanted

            act.preload_act_table_set(LOG_EXP)
            act.wait_ge(ld_const, LD_CONST)
            act.wait_ge(s["posf_made"], 1)
            A(Aneg[:], s128[:, C_ALOG:C_ALOG + CHUNKS * STATE], ACT.Exp).then_inc(s["a_log_exp"], 1)

            def f_tok(g):
                P = tile("tok", g)
                if g >= 3:
                    act.wait_ge(s["h2_made"], g - 2)
                A(h0[:, g % 3].rearrange("p m t -> p (m t)"), P[0:HALF, 0:2 * TOK], ACT.Copy).then_inc(s["h0_made"], 1)

            def f_centre(g):
                P = tile("c1", g)
                if g:
                    act.wait_ge(s["xin_made"], g)
                A(xc1[:].rearrange("p m t -> p (m t)"), P[0:HALF, 0:2 * TOK], ACT.Copy)
                A(sq1[:].rearrange("p m t -> p (m t)"), P[0:HALF, 0:2 * TOK], ACT.Square).then_inc(s["xc1_made"], 1)

            def f_variance(g):
                P = tile("v1", g)
                A(rs1[:, 0], P[0:HALF, 0:TOK], ACT.Ln, bias=eps[0:HALF, :]).then_inc(s["rln1"], 1)
                act.wait_ge(s["rln1"], g + 1)
                A(rs1[:, 1], rs1[:, 0], ACT.Exp, scale=-0.5).then_inc(s["rs1_made"], 1)

            def f_in(g, d):
                P = tile(f"in{d}", g)
                for m in range(2):
                    src = P[0:HALF, m * TOK:(m + 1) * TOK].rearrange("p (b l) -> p b l", b=GROUP)
                    dst = xfb[:, m, d] if d == 0 else xfb[:, m, d, :, ::-1]
                    A(dst, src, ACT.Identity, bias=s96[:, S_INB + 2 * d + m:][:, 0:1]).then_inc(s["xfb_made"], 1)

            def f_xc(g, c):
                if g == 0:
                    act.wait_ge(s["pads_made"], 1)
                P = tile(f"xc{c}", g)
                if g:
                    act.wait_ge(s["conv_made"], CHUNKS * (g - 1) + c + 1)
                A(xpad[:, c, :, TAPS - 1:], P[:, 0:STOK].rearrange("p (q l) -> p q l", q=SEQS), ACT.Copy)\
                    .then_inc(s["xpad_made"], 1)

            def f_z(g, c):
                P = tile(f"z{c}", g)
                if g >= 2:
                    act.wait_ge(s["y_gated"], CHUNKS * (g - 2) + c + 1)
                A(sz[:, g % 2, c], P[:, 0:STOK], ACT.Silu).then_inc(s["sz_made"], 1)

            def f_u(g, c):
                act.wait_ge(s["conv_made"], CHUNKS * g + c + 1)
                if g >= 2:
                    act.wait_ge(s["y_skip"], CHUNKS * (g - 2) + c + 1)
                A(u[:, g % 2, c], conv[:, c], ACT.Silu, bias=s128[:, C_CB + c:C_CB + c + 1]).then_inc(s["u_made"], 1)

            def f_xp(g):
                P = tile("xp", g)
                if g:
                    last = f"bc{BCR // BCP - 1}", g - 1, BCP - 1
                    act.wait_ge(full[BANK[last]], FILL[last])
                A(bc3[:], P[0:3 * BCR, 0:STOK], ACT.Copy)
                A(bcf[:], P[0:XPO, 0:STOK], ACT.Copy).then_inc(s["bcf_made"], 1)

            def f_dt(g, c):
                if g:
                    act.wait_ge(s["a_ready"], UNITS * g)
                if g >= 3:
                    last = f"dn{EXPERTS - 1}", g - 3, 0
                    act.wait_ge(full[BANK[last]], FILL[last])
                if g == 0:
                    act.wait_ge(s["wf_full"], 1)
                P = tile(f"dt{c}", g)
                bias = s128[:, C_DTB + c:C_DTB + c + 1]
                A(spe[:, c], P[:, 0:STOK], ACT.Abs, bias=bias)
                A(dt[:, c], P[:, 0:STOK], ACT.Relu, bias=bias).then_inc(s["sp_abs"], 1)

            def f_parts(g, c):
                cs = parts_chunks(g, c)
                if cs is None:
                    return
                act.wait_ge(s["sp_abs"], CHUNKS * g + c + 1)
                A(spe[:, cs], spe[:, cs], ACT.Exp, scale=-1.0).then_inc(s["sp_exp"], 1)
                act.wait_ge(s["sp_exp"], parts_count(g, c))
                A(spl[:, cs], spe[:, cs], ACT.Ln, bias=1.0).then_inc(s["sp_log"], 1)
                A(spw[:, cs], spe[:, cs], ACT.Identity, bias=1.0).then_inc(s["sp_one"], 1)
                act.wait_ge(s["sp_log"], parts_count(g, c))
                A(spi[:, cs], spl[:, cs], ACT.Exp, scale=-1.0).then_inc(s["sp_parts"], 1)

            def bc(g, p):
                half = BCP * p // (2 * NH)
                if g and BCP * p % NH == 0:
                    is_b = BCP * p % (2 * NH) == 0
                    act.wait_ge(s["b_made" if is_b else "p_made"], UNITS * (g - 1) + CHUNKS * (half + 1))
                for i in range(BCP):
                    P = tile(f"bc{p}", g, i)
                    A(BC[:, half, (BCP * p + i) % (2 * NH)], P[:, 0:STOK], ACT.Copy).then_inc(s["bc_made"], 1)

            def ahead(ug):
                g, k = ug // UNITS, ug % UNITS
                half, c = k // CHUNKS, k % CHUNKS
                if ug == 0:
                    act.wait_ge(s["a_made"], 1)
                if half == 0:
                    act.wait_ge(s["dt_made"], CHUNKS * g + c + 1)
                if ug >= AB:
                    act.wait_ge(s["h_made"], ug - AB + 1)
                for j in range(NH):
                    n = c * STATE + half * NH + j
                    last = A(a[:, ug % AB, j, :, 1:LEN], dt[:, c].rearrange("p (q l) -> p q l", q=SEQS)[:, :, 1:LEN],
                             ACT.Exp, scale=Aneg[:, n:n + 1])
                last.then_inc(s["a_ready"], 1)

            def y_copy(g, c):
                act.wait_ge(s["yT_full"], UNITS * g + CHUNKS + c + 1)
                if CHUNKS * g + c:
                    n = CHUNKS * g + c - 1
                    last = f"y{n % CHUNKS}", n // CHUNKS, 0
                    act.wait_ge(full[BANK[last]], FILL[last])
                A(yTs[0:BLOCKS[0][1], 0:2], YT[c][0:BLOCKS[0][1], 0:2], ACT.Copy)
                A(yTs[0:BLOCKS[2][1], 2], YT[c][0:BLOCKS[2][1], 2], ACT.Copy).then_inc(s["yT_copied"], 1)

            def b_mo(g):
                P = tile("mo", g)
                if g:
                    act.wait_ge(s["t2_made"], g)
                for m in range(2):
                    A(h1[:, m], P[0:HALF, m * TOK:(m + 1) * TOK], ACT.Identity, bias=s96[:, S_OUTB + m:][:, 0:1])\
                        .then_inc(s["mo_made"], 1)

            def b_centre(g, which):
                P = tile(f"c{2 + which}", g)
                n = 2 * g + which
                if n:
                    act.wait_ge(s["t2_made" if which == 0 else "h2_made"], g if which == 0 else g + 1)
                A(xc2[:].rearrange("p m t -> p (m t)"), P[0:HALF, 0:2 * TOK], ACT.Copy)
                A(sq2[:].rearrange("p m t -> p (m t)"), P[0:HALF, 0:2 * TOK], ACT.Square).then_inc(s["xc2_made"], 1)

            def b_variance(g, which):
                P = tile(f"v{2 + which}", g)
                A(rs2[:, 0], P[0:HALF, 0:TOK], ACT.Ln, bias=eps[0:HALF, :]).then_inc(s["rln2"], 1)
                act.wait_ge(s["rln2"], 2 * g + which + 1)
                A(rs2[:, 1], rs2[:, 0], ACT.Exp, scale=-0.5).then_inc(s["rs2_made"], 1)

            def b_logits(g):
                P = tile("gate", g)
                if g:
                    act.wait_ge(s["w_made"], g)
                A(gl[:].rearrange("p b e -> p (b e)"), P[:, 0:GROUP * EXPERTS], ACT.Copy, scale=1.0 / LEN)\
                    .then_inc(s["logits_made"], 1)

            def b_gate(g):
                act.wait_ge(s["gate_in"], g + 1)
                A(ge_[:], gl[:], ACT.Exp).then_inc(s["gate_exp"], 1)

            def b_up(g, i):
                if i == 0:
                    act.wait_ge(s["dt_made"], CHUNKS * min(g + 3, GROUPS))
                if g and i == 0:
                    last = f"dn{EXPERTS - 1}", g - 1, 0
                    act.wait_ge(full[BANK[last]], FILL[last])
                P = tile(f"up{i}", g)
                for j in range(3):
                    f = 3 * i + j
                    A(hid[:, f], P[:, j * TOK:(j + 1) * TOK], ACT.Gelu, bias=s128[:, C_B1 + f:C_B1 + f + 1])\
                        .then_inc(s["hid_raw"], 1)

            steps = {
                "tok": f_tok, "c1": f_centre, "v1": f_variance, "xp": f_xp, "mo": b_mo,
                **{f"dtb{c}": (lambda g, c=c: f_parts(g, c)) for c in range(CHUNKS)},
                "c2": lambda g: b_centre(g, 0), "v2": lambda g: b_variance(g, 0),
                "c3": lambda g: b_centre(g, 1), "v3": lambda g: b_variance(g, 1), "logits": b_logits, "gate": b_gate,
                **{f"in{d}": (lambda g, d=d: f_in(g, d)) for d in range(2)},
                **{f"xc{c}": (lambda g, c=c: f_xc(g, c)) for c in range(CHUNKS)},
                **{f"z{c}": (lambda g, c=c: f_z(g, c)) for c in range(CHUNKS)},
                **{f"u{c}": (lambda g, c=c: f_u(g, c)) for c in range(CHUNKS)},
                **{f"dt{c}": (lambda g, c=c: f_dt(g, c)) for c in range(CHUNKS)},
                **{f"bc{p}": (lambda g, p=p: bc(g, p)) for p in range(BCR // BCP)},
                **{f"y{c}": (lambda g, c=c: y_copy(g, c)) for c in range(CHUNKS)},
                **{f"up{i}": (lambda g, i=i: b_up(g, i)) for i in range(FT // 3)}, "decay": ahead}
            order, held = list(steps_of(ACT_SLOTS)), LOG_EXP
            for n, (st, g) in enumerate(order):
                steps[st](g)
                held = tables_ahead(held, order[n + 1:])

        @block.vector
        def _(dve):
            V = nc.vector
            chain = [0]

            def then(ins):
                chain[0] += 1
                ins.then_inc(s["dve_chain"], 1)
                dve.wait_ge(s["dve_chain"], chain[0])

            def tile(st, g, i=0):
                dve.wait_ge(full[BANK[st, g, i]], FILL[st, g, i])
                return PS[BANK[st, g, i]]

            V.memset(eps[:], LN_EPS)
            dve.wait_ge(ld_small, LD_SMALL)
            V.tensor_copy(posf[:, :, 0:1], s96[:, S_CLS:S_CLS + 2].rearrange("p (m o) -> p m o", o=1))
            pos = s96[:, S_POS:S_POS + 74].rearrange("p (m l) -> p m l", m=2)
            V.tensor_tensor(posf[:, :, 1:2], pos[:, :, 0:1], s96[:, S_CT:S_CT + 2].rearrange("p (m o) -> p m o", o=1),
                            ALU.add)
            V.tensor_tensor(posf[:, :, 2:LEN], pos[:, :, 1:37],
                            s96[:, S_TOKB:S_TOKB + 2].rearrange("p (m o) -> p m o", o=1).broadcast_to([HALF, 2, PATCHES]),
                            ALU.add).then_inc(s["posf_made"], 1)
            V.memset(xpad[:, :, :, 0:TAPS - 1], 0.0).then_inc(s["pads_made"], 1)
            dve.wait_ge(s["a_log_exp"], 1)
            V.tensor_scalar(Aneg[:], Aneg[:], -1.0, None, ALU.mult).then_inc(s["a_made"], 1)
            for i in range(AB):
                last = V.memset(a[:, i, :, :, 0:1], 0.0)
            then(last)

            def f_wf(g):
                if g == 0:
                    dve.wait_ge(s["wf_full"], 1)
                    for c in range(CHUNKS):
                        last = V.tensor_copy(wf[:, c], YT[c][:, :, :].rearrange("p a b -> p (a b)")[:, 0:DIM])
                    last.then_inc(s["wf_made"], 1)

            def scan1(ug):
                g, half, c = ug // UNITS, ug % UNITS // CHUNKS, ug % CHUNKS
                dve.wait_ge(s["bc_made"], BCR * g + 2 * NH * half + NH)
                if half == 0:
                    dve.wait_ge(s["du_made"], CHUNKS * g + c + 1)
                if ug >= HB:
                    dve.wait_ge(s["yT_full"], ug - HB + 1)
                V.tensor_tensor(hb[:, ug % HB], du[:, c:c + 1].broadcast_to([128, NH, STOK]), BC[:, half, 0:NH], ALU.mult)\
                    .then_inc(s["b_made"], 1)

            def scan2(ug):
                dve.wait_ge(s["b_made"], ug + 1)
                dve.wait_ge(s["a_ready"], ug + 1)
                flat = hb[:, ug % HB].rearrange("p n t -> p (n t)")
                V.tensor_tensor_scan(flat, a[:, ug % AB].rearrange("p n q l -> p (n q l)"), flat, 0.0, ALU.mult, ALU.add)\
                    .then_inc(s["h_made"], 1)

            def scan3(ug):
                g, half = ug // UNITS, ug % UNITS // CHUNKS
                dve.wait_ge(s["bc_made"], BCR * g + 2 * NH * (half + 1))
                dve.wait_ge(s["h_made"], ug + 1)
                V.tensor_tensor(hb[:, ug % HB], hb[:, ug % HB], BC[:, half, NH:2 * NH], ALU.mult).then_inc(s["p_made"], 1)

            def f_conv(g, c):
                dve.wait_ge(s["xpad_made"], CHUNKS * g + c + 1)
                if g:
                    dve.wait_ge(s["dt_made"], CHUNKS * (g - 1) + c + 1)
                C = conv[:, c].rearrange("p (q l) -> p q l", q=SEQS)
                tap = lambda k: (xpad[:, c, :, k:k + LEN], s128[:, C_CW + TAPS * c + k:][:, 0:1])
                then(V.tensor_scalar(C, *tap(0), None, ALU.mult))
                for k in range(1, TAPS):
                    ins = V.scalar_tensor_tensor(C, *tap(k), C, ALU.mult, ALU.add)
                    if k < TAPS - 1:
                        then(ins)
                ins.then_inc(s["conv_made"], 1)

            def f_sp(g, c):
                cs = parts_chunks(g, c)
                if cs is not None:
                    dve.wait_ge(s["sp_one"], parts_count(g, c))
                    V.scalar_tensor_tensor(spw[:, cs], spw[:, cs], -1.0, spe[:, cs], ALU.add, ALU.subtract)\
                        .then_inc(s["sp_err"], 1)

            def y_finish(g, c):
                n = CHUNKS * g + c
                P = tile(f"y{c}", g)
                V.scalar_tensor_tensor(yg[:], u[:, g % 2, c], s128[:, C_D + c:C_D + c + 1], P[:, 0:STOK],
                                       ALU.mult, ALU.add).then_inc(s["y_skip"], 1)
                dve.wait_ge(s["y_skip"], n + 1)
                dve.wait_ge(s["sz_made"], n + 1)
                V.tensor_tensor(yg[:], yg[:], sz[:, g % 2, c], ALU.mult).then_inc(s["y_gated"], 1)
                dve.wait_ge(s["y_gated"], n + 1)
                if g:
                    dve.wait_ge(full[BANK["mo", g - 1, 0]], FILL["mo", g - 1, 0])
                y4 = yg[:].rearrange("p (d b l) -> p d b l", d=2, b=GROUP)
                V.tensor_tensor(ys[:, c].rearrange("p (b l) -> p b l", b=GROUP), y4[:, 0], y4[:, 1, :, ::-1], ALU.add)\
                    .then_inc(s["ys_made"], 1)
                dve.wait_ge(s["ys_made"], n + 1)

            def b_gate(g):
                dve.wait_ge(s["t2_made"], g + 1)
                then(V.reduce_sum(tm[:], t2[:].rearrange("p m (b l) -> p m b l", b=GROUP), AX.X))
                wgt = s96[:, S_WG:S_WG + 6].rearrange("p (m o e) -> p m o e", m=2, o=1)
                for m in range(2):
                    sums = tm[:, m].rearrange("p (b o) -> p b o", o=1).broadcast_to([HALF, GROUP, EXPERTS])
                    last = V.tensor_tensor(tmw[:, m], sums, wgt[:, m].broadcast_to([HALF, GROUP, EXPERTS]), ALU.mult)
                last.then_inc(s["tmw_made"], 1)

            def b_gate2(g):
                dve.wait_ge(s["logits_made"], g + 1)
                bcast = lambda col: gm[:, :, col:col + 1].broadcast_to([128, GROUP, EXPERTS])
                then(V.reduce_max(gm[:, :, 0:1], gl[:], AX.X))
                V.tensor_tensor(gl[:], gl[:], bcast(0), ALU.subtract).then_inc(s["gate_in"], 1)
                dve.wait_ge(s["gate_exp"], g + 1)
                then(V.reduce_sum(gm[:, :, 1:2], ge_[:], AX.X))
                then(V.reciprocal(gm[:, :, 2:3], gm[:, :, 1:2]))
                then(V.tensor_tensor(ge_[:], ge_[:], bcast(2), ALU.mult))
                then(V.reduce_max(gm[:, :, 3:4], ge_[:], AX.X))
                V.tensor_tensor(gl[:], ge_[:], bcast(3), ALU.is_equal).then_inc(s["gate_top"], 1)

            def b_mix(g, e):
                P = tile(f"dn{e}", g)
                dve.wait_ge(s["w_made"], g + 1)
                part = yg[0:HALF, :].rearrange("p (m b l) -> p m b l", m=2, b=GROUP)
                w = wg[0:HALF, :, e:e + 1].broadcast_to([HALF, GROUP, LEN])
                for m in range(2):
                    Y = P[0:HALF, m * TOK:(m + 1) * TOK].rearrange("p (b l) -> p b l", b=GROUP)
                    bias = s96[:, S_B2 + EXPERTS * m + e:][:, 0:1]
                    last = V.scalar_tensor_tensor(part[:, m], Y, bias, w, ALU.add, ALU.mult)
                last.then_inc(s["mix_read"], 1)
                dve.wait_ge(s["mix_read"], EXPERTS * g + e + 1)
                flat = lambda t: t[:].rearrange("p m t -> p (m t)")
                if e < EXPERTS - 1:
                    then(V.tensor_tensor(flat(h2), flat(h2), yg[0:HALF, :], ALU.add))
                else:
                    V.tensor_tensor(flat(res), flat(h2), yg[0:HALF, :], ALU.add).then_inc(s["res_made"], 1)
                    dve.wait_ge(s["res_made"], g + 1)

            small = small_steps(dve, V, then)
            steps = {
                **{st: (lambda g, st=st: small[st](g) if on_vector(st, g) else None) for st in small},
                **{f"conv{c}": (lambda g, c=c: f_conv(g, c)) for c in range(CHUNKS)},
                **{f"sp{c}": (lambda g, c=c: f_sp(g, c)) for c in range(CHUNKS)},
                **{f"y{c}": (lambda g, c=c: y_finish(g, c)) for c in range(CHUNKS)},
                "gate": b_gate, "gate2": b_gate2, "wf": f_wf,
                **{f"mix{e}": (lambda g, e=e: b_mix(g, e)) for e in range(EXPERTS)},
                "scan1": scan1, "scan2": scan2, "scan3": scan3}
            for st, g in steps_of(DVE_SLOTS):
                steps[st](g)

        @block.gpsimd
        def _(pool):
            G = nc.gpsimd
            chain = [0]

            def then(ins):
                chain[0] += 1
                ins.then_inc(s["pool_chain"], 1)
                pool.wait_ge(s["pool_chain"], chain[0])

            steps = small_steps(pool, G, then)
            for st, g in steps_of(POOL_SLOTS):
                if not on_vector(st, g):
                    steps[st](g)


def kernel(**inputs):
    import ml_dtypes
    import numpy as np
    import concourse.bacc as bacc
    from concourse import mybir as _mybir
    from concourse.bass_utils import run_bass_kernel_spmd as run

    I = {k: np.asarray(v) for k, v in inputs.items()}
    f = lambda k: I[k]
    cc = np.ascontiguousarray

    def rows(w, p):
        return cc(w.reshape(w.shape[0] // p, p, -1).transpose(1, 0, 2))

    side = 96 // 16
    x = f("x").reshape(GROUPS, GROUP, 3, side, 16, side, 16).transpose(0, 2, 4, 6, 1, 3, 5)
    x = x.reshape(GROUPS, PK, 128, GROUP * PATCHES).transpose(0, 2, 1, 3)
    col = lambda v: rows(v.reshape(-1, 1), HALF)[:, :, 0]
    small96 = np.concatenate([
        rows(f("L0_tok_pos_embedding")[0].T, HALF).reshape(HALF, -1), col(f("L0_tok_b")), col(f("cls_tok")),
        col(f("L0_tok_class_token")), col(f("L0_attn_bm_in_b")), col(f("L0_attn_bm_out_b")), col(f("L0_attn_ln_g")),
        col(f("L0_attn_ln_b")), rows(f("L0_ffn_Wg").T, HALF).reshape(HALF, -1),
        rows(f("L0_ffn_b2").T, HALF).reshape(HALF, -1)], axis=1)
    ch = lambda v: rows(v.reshape(v.shape[0], -1), 128).reshape(128, -1)
    small128 = np.concatenate([
        ch(f("L0_attn_m_conv_w")), ch(f("L0_attn_m_conv_b")), ch(f("L0_attn_m_dt_b")), ch(f("L0_attn_m_A_log")),
        ch(f("L0_attn_m_D")), ch(f("L0_ffn_b1").reshape(-1))], axis=1)
    eye = np.eye(128, dtype=np.float32)
    consts = np.zeros((128, K_END), np.float32)
    consts[:, K_ID:K_ID + 128] = eye
    consts[:HALF, K_CD:K_CD + HALF] = eye[:HALF, :HALF] - np.float32(1.0 / DIM)
    consts[:HALF, K_CO:K_CO + HALF] = -np.float32(1.0 / DIM)
    consts[:HALF, K_J:K_J + HALF] = np.float32(1.0 / DIM)
    consts[:, K_ONE:K_ONE + 128] = 1.0
    sel = np.zeros((3 * BCR, BCR), ml_dtypes.bfloat16)
    for r in range(3 * BCR):
        sel[r, r % BCR] = 1
    xw = f("L0_attn_m_xproj_w").T
    xw = np.concatenate([xw[:, DT_RANK:]] * 3 + [xw[:, :DT_RANK]], axis=1)
    arrays = {
        "xp": x, "tokw": rows(f("L0_tok_W").T, 128), "small96": small96, "small128": small128, "consts": consts,
        "sel": sel, "w_in": rows(f("L0_attn_bm_in_w").T, HALF), "w_min": rows(f("L0_attn_m_in_w").T, HALF),
        "w_xp": rows(xw, 128), "w_dt": f("L0_attn_m_dt_w").T, "w_out": rows(f("L0_attn_m_out_w"), HALF),
        "w_bmo": rows(f("L0_attn_bm_out_w").T, HALF),
        "w1": rows(f("L0_ffn_W1").transpose(1, 0, 2).reshape(DIM, -1), HALF),
        "w2": rows(f("L0_ffn_W2").reshape(-1, DIM), 128)}
    nc = bacc.Bacc("TRN2", target_bir_lowering=False, num_devices=1)
    arrays = {f"in_{k}": cc(v) for k, v in arrays.items()}
    args = [nc.dram_tensor(k, v.shape, _mybir.dt.from_np(v.dtype), kind="ExternalInput").ap() for k, v in arrays.items()]
    args.append(nc.dram_tensor("out_0", (GROUPS, HALF, 2, TOK), _mybir.dt.float32, kind="ExternalOutput").ap())
    tower(nc, *args)
    r = run(nc, [arrays], core_ids=[0])
    got = r.results[0]["out_0"].reshape(GROUPS, HALF, 2, GROUP, LEN)
    return cc(got.transpose(0, 3, 4, 2, 1).reshape(BATCH, LEN, DIM))
```
